# Optimizing a Trainium2 kernel written in Bass

```python
import numpy as np
import jax
import jax.numpy as jnp

def _softmax(x, axis=-1):
    return jax.nn.softmax(x, axis=axis)

def _gelu(x):
    return jax.nn.gelu(x, approximate=True)

def _silu(x):
    return jax.nn.silu(x)

def _sigmoid(x):
    return jax.nn.sigmoid(x)

def _layernorm(x, axis=-1, eps=1e-05):
    m = jnp.mean(x, axis=axis, keepdims=True)
    v = jnp.var(x, axis=axis, keepdims=True)
    return (x - m) / jnp.sqrt(v + eps)

def _scatter_add(tgt, idx, src, axis=0):
    return tgt.at[idx].add(src)

def _segment_sum(src, seg, n):
    return jax.ops.segment_sum(src, seg, n)
kernel_name = 'mk_gnn_ffn_d1_gnn_r8_61ea5e'

def setup_inputs(seed: int=0):
    np.random.seed(seed)
    _w = jnp.asarray

    def _rec_inputs():
        import jax
        import jax.numpy as jnp
        _gk = jax.random.key(seed)
        x = -0.0006008 + 1.001 * jax.random.normal(jax.random.fold_in(_gk, 1), (12500, 256), jnp.float32)
        src = jax.random.randint(jax.random.fold_in(_gk, 2), (200000,), 0, 12500, jnp.int32)
        dst = jax.random.randint(jax.random.fold_in(_gk, 3), (200000,), 0, 12500, jnp.int32)
        _o = jnp.argsort(dst, stable=True)
        src = src[_o]
        dst = dst[_o]
        return (x, src, dst)
    x, src, dst = _rec_inputs()

    def _L0_gnn_setup():
        import jax, jax.numpy as jnp
        import numpy as np
        N_NODES = 1250
        N_EDGES = 40000
        D_IN = 256
        D_OUT = 256
        NEG_SLOPE = 0.2
        key = jax.random.key(seed)
        ks = jax.random.split(key, 8)
        feature = jax.random.normal(ks[0], (N_NODES, D_IN), dtype=jnp.float32)
        src = jax.random.randint(ks[1], (N_EDGES,), 0, N_NODES, dtype=jnp.int32)
        dst = jax.random.randint(ks[2], (N_EDGES,), 0, N_NODES, dtype=jnp.int32)
        s = 1.0 / np.sqrt(D_IN)
        W_s = jax.random.normal(ks[3], (D_OUT, D_IN), dtype=jnp.float32) * s
        W_t = jax.random.normal(ks[4], (D_OUT, D_IN), dtype=jnp.float32) * s
        W_attn = jax.random.normal(ks[5], (1, D_OUT), dtype=jnp.float32) * (1.0 / np.sqrt(D_OUT))
        W_fc = jax.random.normal(ks[6], (D_OUT, D_IN), dtype=jnp.float32) * s
        b_fc = jnp.zeros((D_OUT,), dtype=jnp.float32)
        return {'feature': feature, 'src': src, 'dst': dst, 'W_s': W_s, 'W_t': W_t, 'W_attn': W_attn, 'W_fc': W_fc, 'b_fc': b_fc}
    _L0_gnn_all = _L0_gnn_setup()
    _L0_gnn_in = {k: v for k, v in _L0_gnn_all.items() if k in ('W_s', 'W_t', 'W_attn', 'W_fc', 'b_fc')}
    del _L0_gnn_all

    def _L0_ffn_setup():
        import jax, jax.numpy as jnp
        import numpy as np
        E, D, H, TOP_K = (6, 256, 256, 2)
        ROUTER_H = D // 2
        key = jax.random.key(seed)
        ks = jax.random.split(key, 12)
        s = 1.0 / np.sqrt(D)
        sh = 1.0 / np.sqrt(H)
        sr = 1.0 / np.sqrt(ROUTER_H)
        return {'features': jax.random.normal(ks[0], (8, 512, D), dtype=jnp.float32), 'router_w1': jax.random.uniform(ks[1], (D, ROUTER_H), jnp.float32, -s, s), 'router_b1': jnp.zeros((ROUTER_H,), jnp.float32), 'router_w2': jax.random.uniform(ks[2], (ROUTER_H, E), jnp.float32, -sr, sr), 'router_b2': jnp.zeros((E,), jnp.float32), 'expert_w1': jax.random.uniform(ks[3], (E, D, H), jnp.float32, -s, s), 'expert_b1': jnp.zeros((E, H), jnp.float32), 'expert_w2': jax.random.uniform(ks[4], (E, H, H), jnp.float32, -sh, sh), 'expert_b2': jnp.zeros((E, H), jnp.float32), 'expert_w3': jax.random.uniform(ks[5], (E, H, D), jnp.float32, -sh, sh), 'expert_b3': jnp.zeros((E, D), jnp.float32)}
    _L0_ffn_all = _L0_ffn_setup()
    _L0_ffn_in = {k: v for k, v in _L0_ffn_all.items() if k in ('router_w1', 'router_b1', 'router_w2', 'router_b2', 'expert_w1', 'expert_b1', 'expert_w2', 'expert_b2', 'expert_w3', 'expert_b3')}
    del _L0_ffn_all
    return {'x': x, 'src': src, 'dst': dst, 'L0_gnn_W_s': _L0_gnn_in['W_s'], 'L0_gnn_W_t': _L0_gnn_in['W_t'], 'L0_gnn_W_attn': _L0_gnn_in['W_attn'], 'L0_gnn_W_fc': _L0_gnn_in['W_fc'], 'L0_gnn_b_fc': _L0_gnn_in['b_fc'], 'L0_ffn_router_w1': _L0_ffn_in['router_w1'], 'L0_ffn_router_b1': _L0_ffn_in['router_b1'], 'L0_ffn_router_w2': _L0_ffn_in['router_w2'], 'L0_ffn_router_b2': _L0_ffn_in['router_b2'], 'L0_ffn_expert_w1': _L0_ffn_in['expert_w1'], 'L0_ffn_expert_b1': _L0_ffn_in['expert_b1'], 'L0_ffn_expert_w2': _L0_ffn_in['expert_w2'], 'L0_ffn_expert_b2': _L0_ffn_in['expert_b2'], 'L0_ffn_expert_w3': _L0_ffn_in['expert_w3'], 'L0_ffn_expert_b3': _L0_ffn_in['expert_b3']}

def reference(x, src, dst, L0_gnn_W_s, L0_gnn_W_t, L0_gnn_W_attn, L0_gnn_W_fc, L0_gnn_b_fc, L0_ffn_router_w1, L0_ffn_router_b1, L0_ffn_router_w2, L0_ffn_router_b2, L0_ffn_expert_w1, L0_ffn_expert_b1, L0_ffn_expert_w2, L0_ffn_expert_b2, L0_ffn_expert_w3, L0_ffn_expert_b3):
    import jax
    import jax.numpy as jnp

    def _L0_gnn_ref(feature, src, dst, W_s, W_t, W_attn, W_fc, b_fc):
        import jax, jax.numpy as jnp
        import numpy as np
        N_NODES = 1250
        N_EDGES = 40000
        D_IN = 256
        D_OUT = 256
        NEG_SLOPE = 0.2
        n = feature.shape[0]
        proj_s = feature @ W_s.T
        proj_t = feature @ W_t.T
        z = proj_s[src] + proj_t[dst]
        z = jnp.where(z >= 0, z, NEG_SLOPE * z)
        e = (z @ W_attn.T)[:, 0]
        m = jax.ops.segment_max(e, src, num_segments=n)
        m = jnp.where(jnp.isfinite(m), m, 0.0)
        e_exp = jnp.exp(e - m[src])
        denom = jax.ops.segment_sum(e_exp, src, num_segments=n)
        alpha = e_exp / denom[src]
        msg = feature[src] * alpha[:, None]
        agg = jax.ops.segment_sum(msg, dst, num_segments=n)
        return agg @ W_fc.T + b_fc

    def _L0_ffn_ref(features, router_w1, router_b1, router_w2, router_b2, expert_w1, expert_b1, expert_w2, expert_b2, expert_w3, expert_b3):
        import jax, jax.numpy as jnp
        import numpy as np
        E, D, H, TOP_K = (6, 256, 256, 2)
        ROUTER_H = D // 2
        rh = jax.nn.relu(features @ router_w1 + router_b1)
        expert_logits = jax.nn.softmax(rh @ router_w2 + router_b2, axis=-1)
        top_w, top_i = jax.lax.top_k(expert_logits, TOP_K)
        routing_weights = jax.nn.softmax(top_w, axis=-1)
        h1 = jax.nn.relu(jnp.einsum('bsd,edh->bseh', features, expert_w1) + expert_b1)
        h2 = jax.nn.relu(jnp.einsum('bseh,ehf->bsef', h1, expert_w2) + expert_b2)
        expert_out = jnp.einsum('bsef,efo->bseo', h2, expert_w3) + expert_b3
        sel = jnp.take_along_axis(expert_out, top_i[:, :, :, None], axis=2)
        combined = jnp.sum(sel * routing_weights[..., None], axis=2)
        return combined
    x = x + _L0_gnn_ref(_layernorm(x, axis=-1), src, dst, L0_gnn_W_s, L0_gnn_W_t, L0_gnn_W_attn, L0_gnn_W_fc, L0_gnn_b_fc)
    x = x + _L0_ffn_ref(_layernorm(x, axis=-1)[None], L0_ffn_router_w1, L0_ffn_router_b1, L0_ffn_router_w2, L0_ffn_router_b2, L0_ffn_expert_w1, L0_ffn_expert_b1, L0_ffn_expert_w2, L0_ffn_expert_b2, L0_ffn_expert_w3, L0_ffn_expert_b3)[0]
    return x

_drawn_inputs = setup_inputs


def setup_inputs(seed=0):
    import zlib

    import numpy as np

    out = dict(_drawn_inputs(seed))
    spreads = {'L0_gnn_b_fc': (0.0, 0.1),
     'L0_ffn_router_b1': (0.0, 0.1),
     'L0_ffn_router_b2': (0.0, 0.1),
     'L0_ffn_expert_b1': (0.0, 0.717),
     'L0_ffn_expert_b2': (0.0, 0.304),
     'L0_ffn_expert_b3': (0.0, 0.1)}
    factors = {}
    for name, (base, spread) in spreads.items():
        noise = np.random.default_rng([zlib.crc32(name.encode()), seed]).standard_normal(out[name].shape)
        drawn = base * np.exp(spread * noise) if base else spread * noise
        out[name] = jnp.asarray(drawn.astype(out[name].dtype))
    for name, factor in factors.items():
        out[name] = (out[name] * factor).astype(out[name].dtype)
    return out
```

```python
from contextlib import ExitStack

import concourse.bass as bass
from concourse import mybir

F32, I32 = mybir.dt.float32, mybir.dt.int32
ALU, ACT, AX = mybir.AluOpType, mybir.ActivationFunctionType, mybir.AxisListType

P = 128
D = 256
KD = D // P
EXPERTS = 6
SLOTS = 18
WIN = P * SLOTS
PAIRS = SLOTS // 2
SUBS = 3
SUB_SLOTS = SLOTS // SUBS
FW = D + 2
PIECE = 64
BIG = 1.0e30
RANGE_MAX = 60.0
EPS = 1e-5
NEG_SLOPE = 0.2


def gat_moe(nc, a, out, dbg=None):
    n_edges, edge_rows = a["n_edges"], 125
    nodes = a["x"].shape[0]
    blocks = nodes // P
    groups = blocks // 2
    windows = blocks * SLOTS
    x_g = a["x"].rearrange("(g h p) c -> g p h c", h=2, p=P)
    out_g = out.rearrange("(g h p) c -> g p h c", h=2, p=P)

    feat = nc.dram_tensor("feat_table", [nodes, FW], F32, kind="Internal").ap()
    ps_table = nc.dram_tensor("ps_table", [nodes, D], F32, kind="Internal").ap()
    pt_table = nc.dram_tensor("pt_table", [nodes, D], F32, kind="Internal").ap()
    starts = nc.dram_tensor("window_starts", [1, blocks], I32, kind="Internal").ap()

    root = ExitStack()

    def tile(name, shape, dt=F32, on=root):
        return on.enter_context(nc.sbuf_tensor(name, shape, dt))

    def bank(name, on, shape=(P, 512)):
        return on.enter_context(nc.psum_tensor(name, list(shape), F32))

    def sem(name, on):
        return on.enter_context(nc.semaphore(name))

    ticks = root.enter_context(nc.semaphore("ticks"))

    def hold(engine, semaphore, value):
        engine.wait_ge(semaphore, value)
        engine.sem_inc(ticks, 1)

    def load_window(engine, start, idx, dst_cols, loaded):
        for to, of in ((idx, a["src"]), (dst_cols, a["dst"])):
            engine.dma_start(to, of[bass.ds(start, WIN)].rearrange("(p k) -> p k", k=SLOTS)).then_inc(loaded, 16)

    with root:
        iota_i = tile("iota_i", [P, P], I32)
        iota = tile("iota", [P, P])
        block_base_i = tile("block_base_i", [P, blocks], I32)
        block_base = tile("block_base", [P, blocks])
        node_id_i = tile("node_id_i", [P, blocks], I32)
        node_id = tile("node_id", [P, blocks])
        ident = tile("ident", [P, P])
        ones = tile("ones", [P, P])
        w_attn = tile("w_attn", [P, D])
        w_sign = tile("w_sign", [P, D])
        b_fc = tile("b_fc", [P, D])
        rb2 = tile("rb2", [P, EXPERTS])
        w_st = tile("w_st", [P, KD, 2 * D])
        w_fc = tile("w_fc", [P, KD, D])
        rw1 = tile("rw1", [P, KD, P])
        rb1 = tile("rb1", [P, 1])
        rw2 = tile("rw2", [P, EXPERTS])
        ew1 = tile("ew1", [P, EXPERTS * KD, D])
        ew2 = tile("ew2", [P, EXPERTS * KD, D])
        ew3 = tile("ew3", [P, EXPERTS * KD, D])
        eb1 = tile("eb1", [P, EXPERTS * KD])
        eb2 = tile("eb2", [P, EXPERTS * KD])
        eb3 = tile("eb3", [EXPERTS, D])
        e_all = tile("e_all", [P, windows])
        valid_all = tile("valid_all", [P, windows])
        fits = tile("fits", [P, 1], I32)
        shift = tile("shift", [P, 3])

        with ExitStack() as s:
            weights = sem("weights", s)
            counted = sem("counted", s)
            made = sem("made", s)
            sign_ok = sem("sign_ok", s)
            loads = [
                (w_attn[:, :], a["w_attn"].partition_broadcast(P)), (b_fc[:, :], a["b_fc"].partition_broadcast(P)),
                (rb2[:, :], a["rb2"].partition_broadcast(P)),
                (w_st[:, :, :], a["w_st"].rearrange("(k p) n -> p k n", p=P)),
                (w_fc[:, :, :], a["w_fc"].rearrange("(k p) n -> p k n", p=P)),
                (rw1[:, :, :], a["rw1"].rearrange("(k p) n -> p k n", p=P)),
                (rb1[:, :], a["rb1"]), (rw2[:, :], a["rw2"]),
                (ew1[:, :, :], a["ew1"].rearrange("e (k p) n -> p (e k) n", p=P)),
                (ew2[:, :, :], a["ew2"].rearrange("e (k p) n -> p (e k) n", p=P)),
                (ew3[:, :, :], a["ew3"].rearrange("e (k p) n -> p (e k) n", p=P)),
                (eb1[:, :], a["eb1"]), (eb2[:, :], a["eb2"]), (eb3[:, :], a["eb3"]),
            ]
            with nc.Block() as block:
                @block.sync
                def _(sp):
                    for to, of in loads:
                        sp.dma_start(to, of).then_inc(weights, 16)
                    sp.wait_ge(weights, 16 * len(loads))

                @block.gpsimd
                def _(gp):
                    gp.iota(iota_i[:, :], [[1, P]], base=0, channel_multiplier=0).then_inc(counted, 1)
                    gp.iota(block_base_i[:, :], [[P, blocks]], base=0, channel_multiplier=0).then_inc(counted, 1)
                    gp.iota(node_id_i[:, :], [[P, blocks]], base=0, channel_multiplier=1).then_inc(counted, 1)
                    gp.memset(ident[:, :], 0.0).then_inc(made, 1)
                    gp.memset(ones[:, :], 1.0)
                    gp.wait_ge(made, 1)
                    gp.affine_select(out=ident[:, :], in_=ident[:, :], compare_op=ALU.not_equal, fill=1.0,
                                     base=0, pattern=[[-1, P]], channel_multiplier=1)

                @block.vector
                def _(dve):
                    dve.wait_ge(counted, 3)
                    dve.tensor_copy(iota[:, :], iota_i[:, :])
                    dve.tensor_copy(block_base[:, :], block_base_i[:, :])
                    dve.tensor_copy(node_id[:, :], node_id_i[:, :])
                    dve.wait_ge(weights, 16 * len(loads))
                    dve.tensor_scalar(w_sign[:, :], w_attn[:, :], 0.0, 2.0, ALU.is_ge, ALU.mult).then_inc(sign_ok, 1)
                    dve.tensor_tensor(w_st[:, :, :].rearrange("p k (t n) -> p (k t) n", t=2),
                                      w_st[:, :, :].rearrange("p k (t n) -> p (k t) n", t=2),
                                      w_attn[:, :].unsqueeze(1).to_broadcast([P, 2 * KD, D]), ALU.mult)
                    dve.wait_ge(sign_ok, 1)
                    dve.tensor_scalar(w_sign[:, :], w_sign[:, :], -1.0, None, ALU.add)

        per_row = n_edges // edge_rows
        pieces = per_row // PIECE
        with ExitStack() as s:
            dst_rows = tile("dst_rows", [edge_rows, per_row], I32, s)
            last_f = tile("last_f", [edge_rows, pieces], F32, s)
            below = tile("below", [edge_rows, blocks, pieces], F32, s)
            below_sum = tile("below_sum", [edge_rows, blocks], F32, s)
            piece_f = tile("piece_f", [blocks, 1], F32, s)
            piece_i = tile("piece_i", [blocks, 1], I32, s)
            piece_row = tile("piece_row", [blocks, PIECE], I32, s)
            first_node = tile("first_node", [blocks, 1], F32, s)
            inside = tile("inside", [blocks, PIECE], F32, s)
            inside_sum = tile("inside_sum", [blocks, 1], F32, s)
            start_f = tile("start_f", [blocks, 1], F32, s)
            start_i = tile("start_i", [blocks, 1], I32, s)
            first_i = tile("first_i", [P, 1], I32, s)
            piece_count = bank("piece_count", s)
            dst_in, last_ok, cmp_ok, sum_ok = (sem(n, s) for n in ("dst_in", "last_ok", "cmp_ok", "sum_ok"))
            count_ok, pf_ok, pi_ok, row_in = (sem(n, s) for n in ("count_ok", "pf_ok", "pi_ok", "row_in"))
            first_ok, in_ok, sf_ok, start_ok, stored = (
                sem(n, s) for n in ("first_ok", "in_ok", "sf_ok", "start_ok", "stored"))
            with nc.Block() as block:
                @block.sync
                def _(sp):
                    sp.dma_start(dst_rows[:, :], a["dst"][0:n_edges].rearrange("(p c) -> p c", p=edge_rows)).then_inc(dst_in, 16)
                    sp.wait_ge(start_ok, 1)
                    sp.dma_start(starts.rearrange("a b -> b a"), start_i[:, :]).then_inc(stored, 16)
                    sp.wait_ge(stored, 16)

                @block.gpsimd
                def _(gp):
                    gp.iota(first_i[:, :], [[0, 1]], base=0, channel_multiplier=P).then_inc(first_ok, 1)
                    gp.wait_ge(pi_ok, 1)
                    gp.indirect_dma_start(piece_row[:, :], None, a["dst"].rearrange("(r c) -> r c", c=PIECE),
                                          bass.IndirectOffsetOnAxis(ap=piece_i[:, :], axis=0)).then_inc(row_in, 16)

                @block.tensor
                def _(pe):
                    pe.wait_ge(sum_ok, 1)
                    pe.matmul(piece_count[0:blocks, 0:1], below_sum[:, :], ones[0:edge_rows, 0:1],
                              start=True, stop=True).then_inc(count_ok, 1)

                @block.vector
                def _(dve):
                    dve.wait_ge(dst_in, 16)
                    dve.tensor_copy(last_f[:, :], dst_rows[:, PIECE - 1::PIECE]).then_inc(last_ok, 1)
                    dve.wait_ge(last_ok, 1)
                    dve.tensor_tensor(below[:, :, :], last_f[:, :].unsqueeze(1).to_broadcast([edge_rows, blocks, pieces]),
                                      block_base[0:edge_rows, :].unsqueeze(2).to_broadcast([edge_rows, blocks, pieces]),
                                      ALU.is_lt).then_inc(cmp_ok, 1)
                    dve.wait_ge(cmp_ok, 1)
                    dve.tensor_reduce(below_sum[:, :], below[:, :, :], AX.X, ALU.add).then_inc(sum_ok, 1)
                    dve.wait_ge(count_ok, 1)
                    dve.tensor_copy(piece_f[:, :], piece_count[0:blocks, 0:1]).then_inc(pf_ok, 1)
                    dve.wait_ge(pf_ok, 1)
                    dve.tensor_copy(piece_i[:, :], piece_f[:, :]).then_inc(pi_ok, 1)
                    dve.wait_ge(first_ok, 1)
                    dve.tensor_copy(first_node[:, :], first_i[0:blocks, :]).then_inc(last_ok, 1)
                    dve.wait_ge(last_ok, 2)
                    dve.wait_ge(row_in, 16)
                    dve.tensor_scalar(inside[:, :], piece_row[:, :], first_node[:, :], None, ALU.is_lt).then_inc(in_ok, 1)
                    dve.wait_ge(in_ok, 1)
                    dve.tensor_reduce(inside_sum[:, :], inside[:, :], AX.X, ALU.add).then_inc(in_ok, 1)
                    dve.wait_ge(in_ok, 2)
                    dve.scalar_tensor_tensor(start_f[:, :], piece_f[:, :], float(PIECE), inside_sum[:, :],
                                             ALU.mult, ALU.add).then_inc(sf_ok, 1)
                    dve.wait_ge(sf_ok, 1)
                    dve.tensor_copy(start_i[:, :], start_f[:, :]).then_inc(start_ok, 1)

        with ExitStack() as s:
            x_in = [tile(f"x_in{h}", [P, D], F32, s) for h in range(2)]
            f = [tile(f"f{h}", [P, D], F32, s) for h in range(2)]
            f_t = [tile(f"f_t{h}", [P, KD, P], F32, s) for h in range(2)]
            proj = [tile(f"proj{h}", [P, 2 * D], F32, s) for h in range(2)]
            stats = [tile(f"stats{h}", [P, 6], F32, s) for h in range(2)]
            moments = [tile(f"moments{h}", [P, 2], F32, s) for h in range(2)]
            std = [tile(f"std{h}", [P, 1], F32, s) for h in range(2)]
            rstd = [tile(f"rstd{h}", [P, 1], F32, s) for h in range(2)]
            turned = [bank(f"turned{h}", s) for h in range(2)]
            product = [bank(f"product{h}", s) for h in range(2)]
            x_loaded = [sem(f"x_loaded{h}", s) for h in range(2)]
            f_stored = [sem(f"f_stored{h}", s) for h in range(2)]
            proj_stored = [sem(f"proj_stored{h}", s) for h in range(2)]
            stats_ok, moments_ok, var_ok, std_ok, rstd_ok, f_ok, turned_ok, ft_ok, product_ok, proj_ok = (
                sem("p_" + n, s) for n in ("stats", "moments", "var", "std", "rstd", "f", "turned", "ft", "product", "proj"))

            def rows_of(table, g, h):
                return table.rearrange("(g h p) c -> g h p c", h=2, p=P)[bass.ds(g, 1), h, :, :].rearrange("a p c -> (a p) c")

            with nc.Block() as block:
                @block.sync
                def _(sp):
                    def step(g, first):
                        for h in range(2):
                            if not first:
                                sp.wait_ge(f_ok, 2 * g + h - 1)
                            sp.dma_start(x_in[h][:, :], rows_of(a["x"], g, h)).then_inc(x_loaded[h], 16)
                        for h in range(2):
                            sp.wait_ge(f_ok, 2 * g + h + 1)
                            sp.dma_start(rows_of(feat[:, 0:D], g, h), f[h][:, :]).then_inc(f_stored[h], 16)
                    step(0, True)
                    with sp.Fori(1, groups) as g:
                        step(g, False)
                    for h in range(2):
                        sp.wait_ge(f_stored[h], 16 * groups)

                @block.vector
                def _(dve):
                    def step(g, first):
                        for h in range(2):
                            n = 2 * g + h
                            dve.wait_ge(x_loaded[h], 16 * (g + 1))
                            dve.bn_stats(stats[h][:, :], x_in[h][:, :]).then_inc(stats_ok, 1)
                            hold(dve, stats_ok, n + 1)
                            dve.bn_aggr(moments[h][:, :], stats[h][:, :]).then_inc(moments_ok, 1)
                            dve.wait_ge(moments_ok, n + 1)
                            dve.tensor_scalar(std[h][:, :], moments[h][:, 1:2], EPS, None, ALU.add).then_inc(var_ok, 1)
                        for h in range(2):
                            n = 2 * g + h
                            dve.wait_ge(std_ok, n + 1)
                            dve.reciprocal(rstd[h][:, :], std[h][:, :]).then_inc(rstd_ok, 1)
                            dve.wait_ge(rstd_ok, n + 1)
                            if not first:
                                dve.wait_ge(f_stored[h], 16 * g)
                                dve.wait_ge(turned_ok, n - 1)
                            dve.tensor_scalar(f[h][:, :], x_in[h][:, :], moments[h][:, 0:1], rstd[h][:, :],
                                              ALU.subtract, ALU.mult).then_inc(f_ok, 1)
                    step(0, True)
                    with dve.Fori(1, groups) as g:
                        step(g, False)

                @block.tensor
                def _(pe):
                    def step(g, first):
                        for h in range(2):
                            n = 2 * g + h
                            pe.wait_ge(f_ok, n + 1)
                            if not first:
                                pe.wait_ge(ft_ok, n - 1)
                            for k in range(KD):
                                last = pe.transpose(turned[h][:, k * P:(k + 1) * P], f[h][:, k * P:(k + 1) * P], ident[:, :])
                            last.then_inc(turned_ok, 1)
                        for h in range(2):
                            n = 2 * g + h
                            pe.wait_ge(ft_ok, n + 1)
                            if not first:
                                pe.wait_ge(proj_ok, n - 1)
                            for k in range(KD):
                                last = pe.matmul(product[h][:, :], f_t[h][:, k, :], w_st[:, k, :], start=k == 0, stop=k == KD - 1)
                            last.then_inc(product_ok, 1)
                    step(0, True)
                    with pe.Fori(1, groups) as g:
                        step(g, False)

                @block.scalar
                def _(act):
                    def step(g, first):
                        for h in range(2):
                            n = 2 * g + h
                            act.wait_ge(var_ok, n + 1)
                            act.activation(std[h][:, :], std[h][:, :], ACT.Sqrt).then_inc(std_ok, 1)
                        for h in range(2):
                            n = 2 * g + h
                            act.wait_ge(turned_ok, n + 1)
                            act.activation(f_t[h][:, :, :], turned[h][:, 0:D].rearrange("p (k n) -> p k n", k=KD), ACT.Copy).then_inc(ft_ok, 1)
                        for h in range(2):
                            n = 2 * g + h
                            act.wait_ge(product_ok, n + 1)
                            if not first:
                                act.wait_ge(proj_stored[h], 32 * g)
                            act.activation(proj[h][:, :], product[h][:, :], ACT.Copy).then_inc(proj_ok, 1)
                        for h in range(2):
                            n = 2 * g + h
                            act.wait_ge(proj_ok, n + 1)
                            act.dma_start(rows_of(ps_table, g, h), proj[h][:, 0:D]).then_inc(proj_stored[h], 16)
                            act.dma_start(rows_of(pt_table, g, h), proj[h][:, D:2 * D]).then_inc(proj_stored[h], 16)
                    step(0, True)
                    with act.Fori(1, groups) as g:
                        step(g, False)
                    for h in range(2):
                        act.wait_ge(proj_stored[h], 32 * groups)
        if dbg is not None and dbg(nc, locals(), "project"):
            return

        pair_ring, z_ring = 6, 6
        with ExitStack() as s:
            idx = [tile(f"sc_idx{h}", [P, SLOTS], I32, s) for h in range(2)]
            dst_cols = [tile(f"sc_dst{h}", [P, SLOTS], I32, s) for h in range(2)]
            dst_row = [tile(f"sc_dst_row{h}", [P, WIN], I32, s) for h in range(2)]
            pt_block = [tile(f"pt_block{h}", [P, D], F32, s) for h in range(2)]
            one_hot = [tile(f"one_hot{h}", [P, WIN], F32, s) for h in range(2)]
            local = [tile(f"local{h}", [P, SLOTS], F32, s) for h in range(2)]
            at_least = [tile(f"at_least{h}", [P, SLOTS], F32, s) for h in range(2)]
            ps_rows = [tile(f"ps_rows{r}", [P, 2, D], F32, s) for r in range(pair_ring)]
            z = [tile(f"z{r}", [P, 2, D], F32, s) for r in range(z_ring)]
            plain = tile("plain", [P, windows], F32, s)
            pt_rows = [bank(f"pt_rows{r}", s) for r in range(z_ring)]
            loaded = [sem(f"sc_loaded{h}", s) for h in range(2)]
            gathered = [sem(f"sc_gathered{r}", s) for r in range(pair_ring)]
            all_ok = sem("sc_all", s)
            local_ok, least_ok, one_hot_ok, pt_ok, sum_ok, abs_ok, dot_ok = (
                sem("sc_" + n, s) for n in ("local", "least", "one_hot", "pt", "sum", "abs", "dot"))

            with nc.Block() as block:
                @block.sync
                def _(sp):
                    def step(g, first):
                        for h in range(2):
                            b = 2 * g + h
                            start = sp.value_load(starts[0:1, bass.ds(b, 1)], min_val=0, max_val=n_edges)
                            if not first:
                                hold(sp, sum_ok, 2 * PAIRS * g + PAIRS * (h - 1))
                            load_window(sp, start, idx[h][:, :], dst_cols[h][:, :], loaded[h])
                            sp.dma_start(dst_row[h][:, :], a["dst"][bass.ds(start, WIN)].partition_broadcast(P)).then_inc(loaded[h], 16)
                            sp.dma_start(pt_block[h][:, :], pt_table[bass.ds(b * P, P), :]).then_inc(loaded[h], 16)
                    step(0, True)
                    with sp.Fori(1, groups) as g:
                        step(g, False)

                @block.gpsimd
                def _(gp):
                    def step(g, first):
                        for q in range(2 * PAIRS):
                            h, r, n = q // PAIRS, q % pair_ring, 2 * PAIRS * g + q
                            if q % PAIRS == 0:
                                hold(gp, loaded[h], 64 * (g + 1))
                            if not first or q >= pair_ring:
                                hold(gp, sum_ok, n - pair_ring + 1)
                            for j in range(2):
                                k = 2 * (q % PAIRS) + j
                                gp.indirect_dma_start(ps_rows[r][:, j, :], None, ps_table,
                                                      bass.IndirectOffsetOnAxis(ap=idx[h][:, k:k + 1], axis=0)).then_inc(gathered[r], 16)
                    step(0, True)
                    with gp.Fori(1, groups) as g:
                        step(g, False)

                @block.tensor
                def _(pe):
                    def step(g, first):
                        for q in range(2 * PAIRS):
                            h, r, n = q // PAIRS, q % z_ring, 2 * PAIRS * g + q
                            if q % PAIRS == 0:
                                pe.wait_ge(loaded[h], 64 * (g + 1))
                                pe.wait_ge(one_hot_ok, 2 * g + h + 1)
                            if not first or q >= z_ring:
                                pe.wait_ge(dot_ok, n - z_ring + 1)
                            for j in range(2):
                                k = 2 * (q % PAIRS) + j
                                last = pe.matmul(pt_rows[r][:, j * D:(j + 1) * D], one_hot[h][:, k::SLOTS], pt_block[h][:, :],
                                                 start=True, stop=True)
                            last.then_inc(pt_ok, 1)
                    step(0, True)
                    with pe.Fori(1, groups) as g:
                        step(g, False)

                @block.scalar
                def _(act):
                    def step(g):
                        for q in range(2 * PAIRS):
                            r, n = q % z_ring, 2 * PAIRS * g + q
                            act.wait_ge(sum_ok, n + 1)
                            act.activation(z[r][:, :, :], z[r][:, :, :], ACT.Abs).then_inc(abs_ok, 1)
                    with act.Fori(0, groups) as g:
                        step(g)

                @block.vector
                def _(dve):
                    def dot(n, r):
                        dve.wait_ge(abs_ok, n + 1)
                        for j in range(2):
                            last = dve.scalar_tensor_tensor(z[r][:, j, :], z[r][:, j, :], (1 - NEG_SLOPE) / 2, w_sign[:, :],
                                                            ALU.mult, ALU.mult, accum_out=e_all[:, bass.ds(2 * n + j, 1)])
                        last.then_inc(dot_ok, 1)

                    def step(g, first):
                        for q in range(2 * PAIRS):
                            h, r, n = q // PAIRS, q % z_ring, 2 * PAIRS * g + q
                            b = 2 * g + h
                            if q % PAIRS == 0:
                                dve.wait_ge(loaded[h], 64 * (g + 1))
                                dve.tensor_scalar(one_hot[h][:, :], dst_row[h][:, :], node_id[:, bass.ds(b, 1)], None,
                                                  ALU.is_equal).then_inc(one_hot_ok, 1)
                                dve.tensor_scalar(local[h][:, :], dst_cols[h][:, :], block_base[:, bass.ds(b, 1)], None,
                                                  ALU.subtract).then_inc(local_ok, 1)
                                dve.wait_ge(local_ok, b + 1)
                                dve.tensor_scalar(at_least[h][:, :], local[h][:, :], 0.0, None, ALU.is_ge).then_inc(least_ok, 1)
                                dve.wait_ge(least_ok, b + 1)
                                dve.scalar_tensor_tensor(valid_all[:, bass.ds(b * SLOTS, SLOTS)], local[h][:, :], float(P),
                                                         at_least[h][:, :], ALU.is_lt, ALU.mult)
                            dve.wait_ge(gathered[q % pair_ring], 32 * (2 * PAIRS // pair_ring * g + q // pair_ring + 1))
                            dve.wait_ge(pt_ok, n + 1)
                            for j in range(2):
                                last = dve.scalar_tensor_tensor(z[r][:, j, :], ps_rows[q % pair_ring][:, j, :], 1.0,
                                                                pt_rows[r][:, j * D:(j + 1) * D], ALU.mult, ALU.add,
                                                                accum_out=plain[:, bass.ds(2 * n + j, 1)])
                            last.then_inc(sum_ok, 1)
                            if not first or q >= 2:
                                dot(n - 2, (q - 2) % z_ring)
                    step(0, True)
                    with dve.Fori(1, groups) as g:
                        step(g, False)
                    for n in (groups * 2 * PAIRS - 2, groups * 2 * PAIRS - 1):
                        dot(n, n % z_ring)
                    dve.drain().then_inc(all_ok, 1)
                    dve.wait_ge(all_ok, 1)
                    dve.scalar_tensor_tensor(e_all[:, :], plain[:, :], (1 + NEG_SLOPE) / 2, e_all[:, :], ALU.mult, ALU.add)

        with ExitStack() as s:
            masked = tile("masked", [P, windows], F32, s)
            gap = tile("gap", [P, windows], F32, s)
            extreme = tile("extreme", [P, 3], F32, s)
            turned_sb = tile("turned_sb", [1, 2], F32, s)
            verdict = tile("verdict", [P, 3], F32, s)
            extremes_t = bank("extremes_t", s)
            spread = bank("spread", s)
            step_ok, found_ok, turned_ok, row_ok, spread_ok = (sem("j_" + n, s) for n in ("step", "found", "turned", "row", "spread"))
            with nc.Block() as block:
                @block.vector
                def _(dve):
                    dve.tensor_scalar(gap[:, :], valid_all[:, :], BIG, -BIG, ALU.mult, ALU.add)
                    dve.tensor_tensor(masked[:, :], e_all[:, :], valid_all[:, :], ALU.mult)
                    dve.tensor_reduce(extreme[:, 2:3], valid_all[:, :], AX.X, ALU.add).then_inc(step_ok, 1)
                    dve.wait_ge(step_ok, 1)
                    dve.tensor_tensor(e_all[:, :], gap[:, :], masked[:, :], ALU.add).then_inc(step_ok, 1)
                    dve.tensor_tensor(masked[:, :], gap[:, :], masked[:, :], ALU.subtract).then_inc(step_ok, 1)
                    dve.wait_ge(step_ok, 3)
                    dve.tensor_reduce(extreme[:, 0:1], e_all[:, :], AX.X, ALU.max).then_inc(found_ok, 1)
                    dve.tensor_reduce(extreme[:, 1:2], masked[:, :], AX.X, ALU.max).then_inc(found_ok, 1)
                    dve.wait_ge(turned_ok, 1)
                    dve.tensor_reduce(turned_sb[:, :], extremes_t[0:1, 0:2 * P].rearrange("a (m n) -> a m n", m=2),
                                      AX.X, ALU.max).then_inc(row_ok, 1)
                    dve.wait_ge(spread_ok, 1)
                    dve.tensor_copy(shift[:, :], spread[:, 0:3]).then_inc(step_ok, 1)
                    dve.wait_ge(step_ok, 4)
                    dve.tensor_tensor(verdict[:, 0:1], shift[:, 0:1], shift[:, 1:2], ALU.add).then_inc(step_ok, 1)
                    dve.tensor_scalar(verdict[:, 1:2], shift[:, 2:3], float(n_edges), None, ALU.is_equal).then_inc(step_ok, 1)
                    dve.wait_ge(step_ok, 6)
                    dve.scalar_tensor_tensor(verdict[:, 2:3], verdict[:, 0:1], RANGE_MAX, verdict[:, 1:2],
                                             ALU.is_le, ALU.mult).then_inc(step_ok, 1)
                    dve.wait_ge(step_ok, 7)
                    dve.tensor_copy(fits[:, :], verdict[:, 2:3])

                @block.tensor
                def _(pe):
                    pe.wait_ge(found_ok, 2)
                    for m in range(2):
                        last = pe.transpose(extremes_t[0:1, m * P:(m + 1) * P], extreme[:, m:m + 1], ident[:, :])
                    last.then_inc(turned_ok, 1)
                    pe.matmul(spread[:, 2:3], ones[:, :], extreme[:, 2:3], start=True, stop=True)
                    pe.wait_ge(row_ok, 1)
                    pe.matmul(spread[:, 0:2], ones[0:1, :], turned_sb[:, :], start=True, stop=True).then_inc(spread_ok, 1)
        if dbg is not None and dbg(nc, locals(), "judge"):
            return

        node_terms = tile("node_terms", [P, blocks, 2])
        with ExitStack() as s:
            src_all = tile("src_all", [P, windows], I32, s)
            part_i = tile("part_i", [P, windows], I32, s)
            src_lo = tile("src_lo", [P, windows], F32, s)
            src_hi = tile("src_hi", [P, windows], F32, s)
            weight = tile("weight", [P, windows], F32, s)
            neg_max = tile("neg_max", [P, 1], F32, s)
            total = tile("total", [P, blocks], F32, s)
            lo_hot = [tile(f"lo_hot{h}", [P, SLOTS, P], F32, s) for h in range(2)]
            hi_hot = [tile(f"hi_hot{h}", [P, SLOTS, blocks], F32, s) for h in range(2)]
            sums = [bank(f"sums{h}", s) for h in range(2)]
            src_in, bits_ok, hi_ok, lo_ok, neg_ok, exp_ok, lo_hot_ok, hi_hot_ok, sums_ok, total_ok, terms_ok, stored = (
                sem("w_" + n, s) for n in ("src", "bits", "hi", "lo", "neg", "exp", "lo_hot", "hi_hot", "sums", "total", "terms", "stored"))
            feat_terms = feat[:, D:D + 2].rearrange("(b p) c -> p b c", p=P)
            with nc.Block() as block:
                def when_it_fits(engine, body):
                    fit = engine.value_load(fits[0:1, 0:1], min_val=0, max_val=1)
                    with engine.If(fit == 1):
                        body(engine)

                @block.sync
                def _(sp):
                    def body(sp):
                        with sp.Fori(0, blocks) as b:
                            start = sp.value_load(starts[0:1, bass.ds(b, 1)], min_val=0, max_val=n_edges)
                            sp.dma_start(src_all[:, bass.ds(b * SLOTS, SLOTS)],
                                         a["src"][bass.ds(start, WIN)].rearrange("(p k) -> p k", k=SLOTS)).then_inc(src_in, 16)
                        sp.wait_ge(terms_ok, 1)
                        sp.dma_start(feat_terms, node_terms[:, :, :]).then_inc(stored, 16)
                        sp.wait_ge(stored, 16)
                    when_it_fits(sp, body)

                @block.scalar
                def _(act):
                    def body(act):
                        act.wait_ge(neg_ok, 1)
                        act.activation(weight[:, :], e_all[:, :], ACT.Exp, bias=neg_max[:, :]).then_inc(exp_ok, 1)
                    when_it_fits(act, body)

                @block.tensor
                def _(pe):
                    def step(b, h, first):
                        pe.wait_ge(lo_hot_ok, b + 1)
                        pe.wait_ge(hi_hot_ok, b + 1)
                        if not first:
                            pe.wait_ge(total_ok, b - 1)
                        for k in range(SLOTS):
                            last = pe.matmul(sums[h][:, 0:blocks], lo_hot[h][:, k, :], hi_hot[h][:, k, :],
                                             start=k == 0, stop=k == SLOTS - 1)
                        last.then_inc(sums_ok, 1)

                    def body(pe):
                        for h in range(2):
                            step(h, h, True)
                        with pe.Fori(1, groups) as g:
                            for h in range(2):
                                step(2 * g + h, h, False)
                    when_it_fits(pe, body)

                @block.vector
                def _(dve):
                    def add_up(b, h):
                        dve.wait_ge(sums_ok, b + 1)
                        dve.wait_ge(total_ok, b + 1)
                        dve.tensor_tensor(total[:, :], total[:, :], sums[h][:, 0:blocks], ALU.add).then_inc(total_ok, 1)

                    def step(b, h, first):
                        if not first:
                            dve.wait_ge(sums_ok, b - 1)
                        dve.tensor_tensor(hi_hot[h][:, :, :],
                                          src_hi[:, bass.ds(b * SLOTS, SLOTS)].unsqueeze(2).to_broadcast([P, SLOTS, blocks]),
                                          iota[:, 0:blocks].unsqueeze(1).to_broadcast([P, SLOTS, blocks]),
                                          ALU.is_equal).then_inc(hi_hot_ok, 1)
                        for k in range(SLOTS):
                            col = b * SLOTS + k
                            last = dve.tensor_scalar(lo_hot[h][:, k, :], iota[:, :], src_lo[:, bass.ds(col, 1)],
                                                     weight[:, bass.ds(col, 1)], ALU.is_equal, ALU.mult)
                        last.then_inc(lo_hot_ok, 1)

                    def body(dve):
                        dve.tensor_scalar(neg_max[:, :], shift[:, 0:1], -1.0, None, ALU.mult).then_inc(neg_ok, 1)
                        dve.memset(total[:, :], 0.0).then_inc(total_ok, 1)
                        dve.wait_ge(src_in, 16 * blocks)
                        dve.tensor_scalar(part_i[:, :], src_all[:, :], 7, None, ALU.logical_shift_right).then_inc(bits_ok, 1)
                        dve.wait_ge(bits_ok, 1)
                        dve.tensor_copy(src_hi[:, :], part_i[:, :]).then_inc(hi_ok, 1)
                        dve.wait_ge(hi_ok, 1)
                        dve.tensor_scalar(part_i[:, :], src_all[:, :], P - 1, None, ALU.bitwise_and).then_inc(bits_ok, 1)
                        dve.wait_ge(bits_ok, 2)
                        dve.tensor_copy(src_lo[:, :], part_i[:, :]).then_inc(lo_ok, 1)
                        dve.wait_ge(lo_ok, 1)
                        dve.wait_ge(exp_ok, 1)
                        step(0, 0, True)
                        step(1, 1, True)
                        add_up(0, 0)
                        add_up(1, 1)
                        with dve.Fori(1, groups) as g:
                            for h in range(2):
                                step(2 * g + h, h, False)
                            for h in range(2):
                                add_up(2 * g + h, h)
                        dve.wait_ge(total_ok, blocks + 1)
                        dve.tensor_scalar(total[:, :], total[:, :], 1e-37, None, ALU.max).then_inc(total_ok, 1)
                        dve.wait_ge(total_ok, blocks + 2)
                        dve.reciprocal(node_terms[:, :, 1:2], total[:, :].unsqueeze(2)).then_inc(total_ok, 1)
                        dve.tensor_copy(node_terms[:, :, 0:1], shift[:, 0:1].unsqueeze(1).to_broadcast([P, blocks, 1])).then_inc(total_ok, 1)
                        dve.wait_ge(total_ok, blocks + 4)
                        dve.sem_inc(terms_ok, 1)
                    when_it_fits(dve, body)
        if dbg is not None and dbg(nc, locals(), "weigh"):
            return

        with ExitStack() as s:
            idx = [tile(f"mx_idx{h}", [P, SLOTS], I32, s) for h in range(2)]
            dst_cols = [tile(f"mx_dst{h}", [P, SLOTS], I32, s) for h in range(2)]
            local = [tile(f"mx_local{h}", [P, SLOTS], F32, s) for h in range(2)]
            alpha = [tile(f"alpha{h}", [P, SLOTS], F32, s) for h in range(2)]
            f_rows = [tile(f"f_rows{h}", [P, SLOTS, FW], F32, s) for h in range(2)]
            alpha_hot = [tile(f"alpha_hot{h}", [P, SLOTS, P], F32, s) for h in range(2)]
            agg = [tile(f"agg{h}", [P, D], F32, s) for h in range(2)]
            agg_t = [tile(f"agg_t{h}", [P, KD, P], F32, s) for h in range(2)]
            x_in = tile("mx_x", [P, 2, D], F32, s)
            x1 = [tile(f"x1_{h}", [P, D], F32, s) for h in range(2)]
            f1 = [tile(f"f1_{h}", [P, D], F32, s) for h in range(2)]
            stats = [tile(f"mx_stats{h}", [P, 6], F32, s) for h in range(2)]
            moments = [tile(f"mx_moments{h}", [P, 2], F32, s) for h in range(2)]
            std = [tile(f"mx_std{h}", [P, 1], F32, s) for h in range(2)]
            rstd = [tile(f"mx_rstd{h}", [P, 1], F32, s) for h in range(2)]
            f1_t = tile("f1_t", [P, KD, 2 * P], F32, s)
            rh_t = tile("rh_t", [P, 2 * P], F32, s)
            logits = tile("logits", [P, 2, 8], F32, s)
            top = tile("top", [P, 2, 8], F32, s)
            top_i = tile("top_i", [P, 2, 8], mybir.dt.uint32, s)
            top_f = tile("top_f", [P, 4], F32, s)
            less_top = tile("less_top", [P, 2, 8], F32, s)
            exps = tile("exps", [P, 2, 8], F32, s)
            norm = tile("norm", [P, 2, 2], F32, s)
            pick = tile("pick", [P, 2, 2, 8], F32, s)
            share = tile("share", [P, 2, 8], F32, s)
            share_t = tile("share_t", [8, 2 * P], F32, s)
            h1_t = tile("h1_t", [P, KD, 2 * P], F32, s)
            h2_t = tile("h2_t", [P, KD, 2 * P], F32, s)
            mixed = tile("mixed", [P, 2, D], F32, s)

            agg_bank = [bank(f"agg_bank{h}", s) for h in range(2)]
            graph_bank = bank("graph_bank", s)
            layer_bank = [bank(f"layer_bank{i}", s) for i in range(3)]
            f1_bank = bank("f1_bank", s)
            router_bank = bank("router_bank", s)

            loaded = [sem(f"mx_loaded{h}", s) for h in range(2)]
            gathered = [sem(f"mx_gathered{h}", s) for h in range(2)]
            local_ok, diff_ok, min_ok, exp_ok, alpha_ok, hot_ok, used = (
                [sem(f"mx_{n}{h}", s) for h in range(2)] for n in ("local", "diff", "min", "exp", "alpha", "hot", "used"))
            agg_ok, agg_turned, agg_t_ok, graph_ok, res_ok, x1_ok, stats_ok, moments_ok, var_ok, std_ok, rstd_ok, f1_ok = (
                [sem(f"mx_{n}{h}", s) for h in range(2)]
                for n in ("agg", "agg_turned", "agg_t", "graph", "res", "x1", "stats", "moments", "var", "std", "rstd", "f1"))
            x_loaded, f1_turned, f1_t_ok, rh_ok, rh_t_ok, logit_ok, share_ok, share_turned, share_t_ok, bias_ok = (
                sem("mx_" + n, s) for n in ("x_loaded", "f1_turned", "f1_t", "rh", "rh_t", "logit", "share",
                                            "share_turned", "share_t", "bias"))
            made_ok = [sem(f"mx_made{i}", s) for i in range(3)]
            kept_ok = [sem(f"mx_kept{i}", s) for i in range(3)]
            out_stored = sem("mx_out_stored", s)
            route = sem("mx_route", s)

            def x_rows(table, g):
                return table[bass.ds(g, 1), :, :, :].rearrange("a p h c -> (a p) h c")

            def window_load(sp, start, h, n, first):
                if not first:
                    hold(sp, gathered[h], SLOTS * 16 * n)
                    hold(sp, local_ok[h], n)
                load_window(sp, start, idx[h][:, :], dst_cols[h][:, :], loaded[h])

            def window_gather(gp, h, n, first):
                hold(gp, loaded[h], 32 * (n + 1))
                for k in range(SLOTS):
                    if not first and k % SUB_SLOTS == 0:
                        hold(gp, used[h], SUBS * n - SUBS + k // SUB_SLOTS + 1)
                    gp.indirect_dma_start(f_rows[h][:, k, :], None, feat,
                                          bass.IndirectOffsetOnAxis(ap=idx[h][:, k:k + 1], axis=0)).then_inc(gathered[h], 16)

            def window_weights(dve, h, n, first, b, score_at):
                dve.wait_ge(loaded[h], 32 * (n + 1))
                if not first:
                    dve.wait_ge(used[h], SUBS * n)
                dve.tensor_scalar(local[h][:, :], dst_cols[h][:, :], block_base[:, bass.ds(b, 1)], None,
                                  ALU.subtract).then_inc(local_ok[h], 1)
                dve.wait_ge(gathered[h], SLOTS * 16 * (n + 1))
                dve.tensor_tensor(alpha[h][:, :].unsqueeze(2), e_all[:, bass.ds(score_at, SLOTS)].unsqueeze(2),
                                  f_rows[h][:, :, D:D + 1], ALU.subtract).then_inc(diff_ok[h], 1)
                dve.wait_ge(diff_ok[h], n + 1)
                dve.tensor_scalar(alpha[h][:, :], alpha[h][:, :], 0.0, None, ALU.min).then_inc(min_ok[h], 1)

            def window_exp(act, h, n):
                act.wait_ge(min_ok[h], n + 1)
                act.activation(alpha[h][:, :], alpha[h][:, :], ACT.Exp).then_inc(exp_ok[h], 1)

            def window_alpha(dve, h, n):
                dve.wait_ge(exp_ok[h], n + 1)
                dve.tensor_tensor(alpha[h][:, :].unsqueeze(2), alpha[h][:, :].unsqueeze(2), f_rows[h][:, :, D + 1:D + 2],
                                  ALU.mult).then_inc(alpha_ok[h], 1)
                dve.wait_ge(alpha_ok[h], n + 1)

            def window_hot(dve, h, sub):
                for k in range(sub * SUB_SLOTS, (sub + 1) * SUB_SLOTS):
                    last = dve.tensor_scalar(alpha_hot[h][:, k, :], iota[:, :], local[h][:, k:k + 1], alpha[h][:, k:k + 1],
                                             ALU.is_equal, ALU.mult)
                last.then_inc(hot_ok[h], 1)

            def window_add(pe, h, n, sub, half):
                if half == 0:
                    pe.wait_ge(hot_ok[h], SUBS * n + sub + 1)
                k0 = sub * SUB_SLOTS + half * (SUB_SLOTS // 2)
                for k in range(k0, k0 + SUB_SLOTS // 2):
                    last = pe.matmul(agg_bank[h][:, 0:D], alpha_hot[h][:, k, :], f_rows[h][:, k, 0:D],
                                     start=k == 0, stop=k == SLOTS - 1)
                if half == 1:
                    last.then_inc(used[h], 1)

            def graph_copy(act, h, g, n):
                act.wait_ge(used[h], SUBS * (n + 1))
                act.activation(agg[h][:, :], agg_bank[h][:, 0:D], ACT.Copy).then_inc(agg_ok[h], 1)

            def graph_turn(pe, h, g):
                pe.wait_ge(agg_ok[h], g + 1)
                for k in range(KD):
                    last = pe.transpose(graph_bank[:, k * P:(k + 1) * P], agg[h][:, k * P:(k + 1) * P], ident[:, :])
                last.then_inc(agg_turned[h], 1)

            def graph_turned(act, h, g):
                act.wait_ge(agg_turned[h], g + 1)
                act.activation(agg_t[h][:, :, :], graph_bank[:, 0:D].rearrange("p (k n) -> p k n", k=KD), ACT.Copy).then_inc(agg_t_ok[h], 1)

            def graph_product(pe, h, g):
                pe.wait_ge(agg_t_ok[h], g + 1)
                for k in range(KD):
                    last = pe.matmul(graph_bank[:, D:2 * D], agg_t[h][:, k, :], w_fc[:, k, :], start=k == 0, stop=k == KD - 1)
                last.then_inc(graph_ok[h], 1)

            def graph_norm(dve, h, g):
                dve.wait_ge(x_loaded, 16 * (g + 1))
                dve.tensor_tensor(x1[h][:, :], x_in[:, h, :], b_fc[:, :], ALU.add).then_inc(res_ok[h], 1)
                dve.wait_ge(graph_ok[h], g + 1)
                dve.wait_ge(res_ok[h], g + 1)
                dve.tensor_tensor(x1[h][:, :], graph_bank[:, D:2 * D], x1[h][:, :], ALU.add).then_inc(x1_ok[h], 1)
                dve.wait_ge(x1_ok[h], g + 1)
                dve.bn_stats(stats[h][:, :], x1[h][:, :]).then_inc(stats_ok[h], 1)
                hold(dve, stats_ok[h], g + 1)
                dve.bn_aggr(moments[h][:, :], stats[h][:, :]).then_inc(moments_ok[h], 1)
                dve.wait_ge(moments_ok[h], g + 1)
                dve.tensor_scalar(std[h][:, :], moments[h][:, 1:2], EPS, None, ALU.add).then_inc(var_ok[h], 1)

            def graph_root(act, h, g):
                act.wait_ge(var_ok[h], g + 1)
                act.activation(std[h][:, :], std[h][:, :], ACT.Sqrt).then_inc(std_ok[h], 1)

            def graph_features(dve, h, g):
                dve.wait_ge(std_ok[h], g + 1)
                dve.reciprocal(rstd[h][:, :], std[h][:, :]).then_inc(rstd_ok[h], 1)
                dve.wait_ge(rstd_ok[h], g + 1)
                dve.tensor_scalar(f1[h][:, :], x1[h][:, :], moments[h][:, 0:1], rstd[h][:, :],
                                  ALU.subtract, ALU.mult).then_inc(f1_ok[h], 1)

            def moe_turn(pe, m):
                for h in range(2):
                    pe.wait_ge(f1_ok[h], m + 1)
                    for k in range(KD):
                        last = pe.transpose(f1_bank[:, (2 * k + h) * P:(2 * k + h + 1) * P], f1[h][:, k * P:(k + 1) * P], ident[:, :])
                last.then_inc(f1_turned, 1)

            def moe_turned(act, m):
                act.wait_ge(f1_turned, m + 1)
                act.activation(f1_t[:, :, :], f1_bank[:, :].rearrange("p (k n) -> p k n", k=KD), ACT.Copy).then_inc(f1_t_ok, 1)

            def router_hidden(pe, m):
                pe.wait_ge(f1_t_ok, m + 1)
                for k in range(KD):
                    last = pe.matmul(router_bank[:, 0:2 * P], rw1[:, k, :], f1_t[:, k, :], start=k == 0, stop=k == KD - 1)
                last.then_inc(rh_ok, 1)

            def router_relu(act, m):
                act.wait_ge(rh_ok, m + 1)
                act.activation(rh_t[:, :], router_bank[:, 0:2 * P], ACT.Relu, bias=rb1[:, :]).then_inc(rh_t_ok, 1)

            def router_logits(pe, m):
                pe.wait_ge(rh_t_ok, m + 1)
                for h in range(2):
                    last = pe.matmul(router_bank[:, 256 + 8 * h:256 + 8 * h + EXPERTS], rh_t[:, h * P:(h + 1) * P], rw2[:, :],
                                     start=True, stop=True)
                last.then_inc(logit_ok, 1)

            ROUTE = 13

            def route_top(dve, m):
                at = ROUTE * m
                dve.wait_ge(logit_ok, m + 1)
                dve.tensor_tensor(logits[:, :, 0:EXPERTS], router_bank[:, 256:272].rearrange("p (h e) -> p h e", h=2)[:, :, 0:EXPERTS],
                                  rb2[:, :].unsqueeze(1).to_broadcast([P, 2, EXPERTS]), ALU.add).then_inc(route, 1)
                hold(dve, route, at + 1)
                for h in range(2):
                    dve.max(top[:, h, :], logits[:, h, :]).then_inc(route, 1)
                dve.wait_ge(route, at + 3)
                dve.tensor_tensor(less_top[:, :, :], logits[:, :, :], top[:, :, 0:1].to_broadcast([P, 2, 8]), ALU.subtract).then_inc(route, 1)

            def route_exp(act, m):
                act.wait_ge(route, ROUTE * m + 4)
                act.activation(exps[:, :, :], less_top[:, :, :], ACT.Exp).then_inc(route, 1)

            def route_probs(dve, m):
                at = ROUTE * m
                dve.wait_ge(route, at + 5)
                dve.tensor_reduce(norm[:, :, 0:1], exps[:, :, :], AX.X, ALU.add).then_inc(route, 1)
                dve.wait_ge(route, at + 6)
                dve.reciprocal(norm[:, :, 1:2], norm[:, :, 0:1]).then_inc(route, 1)
                dve.wait_ge(route, at + 7)
                dve.tensor_tensor(exps[:, :, :], exps[:, :, :], norm[:, :, 1:2].to_broadcast([P, 2, 8]), ALU.mult).then_inc(route, 1)
                hold(dve, route, at + 8)
                for h in range(2):
                    last = dve.max(top[:, h, :], exps[:, h, :])
                last.then_inc(route, 1)
                hold(dve, route, at + 9)
                for h in range(2):
                    last = dve.max_index(top_i[:, h, :], top[:, h, :], exps[:, h, :])
                last.then_inc(route, 1)
                dve.wait_ge(route, at + 10)
                dve.tensor_copy(top_f[:, :].rearrange("p (h t) -> p h t", h=2), top_i[:, :, 0:2])
                dve.tensor_tensor(norm[:, :, 0:1], top[:, :, 1:2], top[:, :, 0:1], ALU.subtract).then_inc(route, 1)

            def route_second(act, m):
                act.wait_ge(route, ROUTE * m + 11)
                act.activation(norm[:, :, 1:2], norm[:, :, 0:1], ACT.Exp).then_inc(route, 1)

            def route_shares(dve, m):
                at = ROUTE * m
                dve.wait_ge(route, at + 12)
                dve.tensor_scalar(norm[:, :, 0:1], norm[:, :, 1:2], 1.0, None, ALU.add).then_inc(route, 1)
                dve.wait_ge(route, at + 13)
                base = SHARE * m
                dve.reciprocal(norm[:, :, 0:1], norm[:, :, 0:1]).then_inc(share_ok, 1)
                dve.tensor_tensor(pick[:, :, :, :].rearrange("p h t e -> p (h t) e"),
                                  top_f[:, :].unsqueeze(2).to_broadcast([P, 4, 8]),
                                  iota[:, 0:8].unsqueeze(1).to_broadcast([P, 4, 8]), ALU.is_equal).then_inc(share_ok, 1)
                dve.wait_ge(share_ok, base + 2)
                dve.tensor_tensor(norm[:, :, 1:2], norm[:, :, 1:2], norm[:, :, 0:1], ALU.mult).then_inc(share_ok, 1)
                dve.wait_ge(share_ok, base + 3)
                for h in range(2):
                    last = dve.tensor_scalar(share[:, h, :], pick[:, h, 0, :], norm[:, h, 0:1], None, ALU.mult)
                last.then_inc(share_ok, 1)
                dve.wait_ge(share_ok, base + 4)
                for h in range(2):
                    last = dve.scalar_tensor_tensor(share[:, h, :], pick[:, h, 1, :], norm[:, h, 1:2], share[:, h, :], ALU.mult, ALU.add)
                last.then_inc(share_ok, 1)

            SHARE = 5

            def bias_turn(pe, m):
                pe.wait_ge(share_ok, SHARE * (m + 1))
                for h in range(2):
                    last = pe.transpose(router_bank[0:8, h * P:(h + 1) * P], share[:, h, :], ident[:, :])
                last.then_inc(share_turned, 1)

            def bias_turned(act, m):
                act.wait_ge(share_turned, m + 1)
                act.activation(share_t[:, :], router_bank[0:8, 0:2 * P], ACT.Copy).then_inc(share_t_ok, 1)

            def bias_product(pe, m):
                pe.wait_ge(share_t_ok, m + 1)
                for h in range(2):
                    last = pe.matmul(f1_bank[:, h * D:(h + 1) * D], share_t[0:EXPERTS, h * P:(h + 1) * P], eb3[:, :], start=True, stop=True)
                last.then_inc(bias_ok, 1)

            def bias_residual(dve, m):
                dve.wait_ge(bias_ok, m + 1)
                dve.wait_ge(out_stored, 16 * m + 16)
                for h in range(2):
                    last = dve.tensor_tensor(mixed[:, h, :], f1_bank[:, h * D:(h + 1) * D], x1[h][:, :], ALU.add)
                last.then_inc(kept_ok[2], 1)

            def expert_up(pe, m, e):
                for half in range(KD):
                    for k in range(KD):
                        last = pe.matmul(layer_bank[0][:, half * D:(half + 1) * D], ew1[:, e * KD + k, half * P:(half + 1) * P],
                                         f1_t[:, k, :], start=k == 0, stop=k == KD - 1)
                last.then_inc(made_ok[0], 1)

            def expert_relu(act, m, e, layer):
                act.wait_ge(made_ok[layer], EXPERTS * m + e + 1)
                to, bias = ((h1_t, eb1), (h2_t, eb2))[layer]
                for half in range(KD):
                    last = act.activation(to[:, half, :], layer_bank[layer][:, half * D:(half + 1) * D], ACT.Relu,
                                          bias=bias[:, e * KD + half:e * KD + half + 1])
                last.then_inc(kept_ok[layer], 1)

            def expert_mid(pe, m, e):
                pe.wait_ge(kept_ok[0], EXPERTS * m + e + 1)
                for half in range(KD):
                    for k in range(KD):
                        last = pe.matmul(layer_bank[1][:, half * D:(half + 1) * D], ew2[:, e * KD + k, half * P:(half + 1) * P],
                                         h1_t[:, k, :], start=k == 0, stop=k == KD - 1)
                last.then_inc(made_ok[1], 1)

            def expert_down(pe, m, e):
                pe.wait_ge(kept_ok[1], EXPERTS * m + e + 1)
                pe.wait_ge(kept_ok[2], (EXPERTS + 1) * m + e + 1)
                for h in range(2):
                    for k in range(KD):
                        last = pe.matmul(layer_bank[2][:, h * D:(h + 1) * D], h2_t[:, k, h * P:(h + 1) * P], ew3[:, e * KD + k, :],
                                         start=k == 0, stop=k == KD - 1)
                last.then_inc(made_ok[2], 1)

            def expert_add(dve, m, e):
                dve.wait_ge(made_ok[2], EXPERTS * m + e + 1)
                dve.wait_ge(kept_ok[2], (EXPERTS + 1) * m + e + 1)
                for h in range(2):
                    last = dve.scalar_tensor_tensor(mixed[:, h, :], layer_bank[2][:, h * D:(h + 1) * D], share[:, h, e:e + 1],
                                                    mixed[:, h, :], ALU.mult, ALU.add)
                last.then_inc(kept_ok[2], 1)

            def moe_store(sp, m):
                sp.wait_ge(kept_ok[2], (EXPERTS + 1) * (m + 1))
                sp.dma_start(x_rows(out_g, m), mixed[:, :, :]).then_inc(out_stored, 16)

            def x_load(sp, g, first):
                if not first:
                    sp.wait_ge(x1_ok[1], g)
                sp.dma_start(x_in[:, :, :], x_rows(x_g, g)).then_inc(x_loaded, 16)

            with nc.Block() as block:
                @block.sync
                def _(sp):
                    def windows_of(g, first):
                        for h in range(2):
                            start = sp.value_load(starts[0:1, bass.ds(2 * g + h, 1)], min_val=0, max_val=n_edges)
                            window_load(sp, start, h, g, first)

                    sp.sem_inc(out_stored, 16)
                    windows_of(0, True)
                    x_load(sp, 0, True)
                    windows_of(1, False)
                    x_load(sp, 1, False)
                    with sp.Fori(1, groups - 1) as g:
                        windows_of(g + 1, False)
                        moe_store(sp, g - 1)
                        x_load(sp, g + 1, False)
                    moe_store(sp, groups - 2)
                    moe_store(sp, groups - 1)
                    sp.wait_ge(out_stored, 16 * groups + 16)

                @block.gpsimd
                def _(gp):
                    for h in range(2):
                        window_gather(gp, h, 0, True)
                    with gp.Fori(1, groups) as g:
                        for h in range(2):
                            window_gather(gp, h, g, False)

                @block.tensor
                def _(pe):
                    def window(g, h):
                        for sub in range(SUBS):
                            for half in range(2):
                                window_add(pe, h, g, sub, half)

                    for h in range(2):
                        window(0, h)
                        graph_turn(pe, h, 0)
                        graph_product(pe, h, 0)
                    with pe.Fori(1, groups) as g:
                        m = g - 1
                        window_add(pe, 0, g, 0, 0)
                        window_add(pe, 0, g, 0, 1)
                        moe_turn(pe, m)
                        window_add(pe, 0, g, 1, 0)
                        router_hidden(pe, m)
                        window_add(pe, 0, g, 1, 1)
                        router_logits(pe, m)
                        expert_up(pe, m, 0)
                        window_add(pe, 0, g, 2, 0)
                        expert_mid(pe, m, 0)
                        window_add(pe, 0, g, 2, 1)
                        bias_turn(pe, m)
                        expert_up(pe, m, 1)
                        graph_turn(pe, 0, g)
                        bias_product(pe, m)
                        expert_down(pe, m, 0)
                        graph_product(pe, 0, g)
                        expert_mid(pe, m, 1)
                        window_add(pe, 1, g, 0, 0)
                        expert_down(pe, m, 1)
                        expert_up(pe, m, 2)
                        window_add(pe, 1, g, 0, 1)
                        expert_mid(pe, m, 2)
                        window_add(pe, 1, g, 1, 0)
                        expert_down(pe, m, 2)
                        expert_up(pe, m, 3)
                        window_add(pe, 1, g, 1, 1)
                        expert_mid(pe, m, 3)
                        window_add(pe, 1, g, 2, 0)
                        expert_down(pe, m, 3)
                        expert_up(pe, m, 4)
                        window_add(pe, 1, g, 2, 1)
                        expert_mid(pe, m, 4)
                        graph_turn(pe, 1, g)
                        expert_down(pe, m, 4)
                        expert_up(pe, m, 5)
                        graph_product(pe, 1, g)
                        expert_mid(pe, m, 5)
                        expert_down(pe, m, 5)
                    m = groups - 1
                    moe_turn(pe, m)
                    router_hidden(pe, m)
                    router_logits(pe, m)
                    for e in range(EXPERTS):
                        expert_up(pe, m, e)
                        expert_mid(pe, m, e)
                        if e == 0:
                            bias_turn(pe, m)
                            bias_product(pe, m)
                        expert_down(pe, m, e)

                @block.scalar
                def _(act):
                    for h in range(2):
                        window_exp(act, h, 0)
                        graph_copy(act, h, 0, 0)
                        graph_turned(act, h, 0)
                        graph_root(act, h, 0)
                    with act.Fori(1, groups) as g:
                        m = g - 1
                        window_exp(act, 0, g)
                        moe_turned(act, m)
                        router_relu(act, m)
                        route_exp(act, m)
                        expert_relu(act, m, 0, 0)
                        route_second(act, m)
                        expert_relu(act, m, 0, 1)
                        graph_copy(act, 0, g, g)
                        bias_turned(act, m)
                        expert_relu(act, m, 1, 0)
                        graph_turned(act, 0, g)
                        window_exp(act, 1, g)
                        expert_relu(act, m, 1, 1)
                        expert_relu(act, m, 2, 0)
                        graph_root(act, 0, g)
                        expert_relu(act, m, 2, 1)
                        expert_relu(act, m, 3, 0)
                        expert_relu(act, m, 3, 1)
                        expert_relu(act, m, 4, 0)
                        graph_copy(act, 1, g, g)
                        expert_relu(act, m, 4, 1)
                        graph_turned(act, 1, g)
                        expert_relu(act, m, 5, 0)
                        expert_relu(act, m, 5, 1)
                        graph_root(act, 1, g)
                    m = groups - 1
                    moe_turned(act, m)
                    router_relu(act, m)
                    route_exp(act, m)
                    expert_relu(act, m, 0, 0)
                    expert_relu(act, m, 0, 1)
                    route_second(act, m)
                    bias_turned(act, m)
                    for e in range(1, EXPERTS):
                        expert_relu(act, m, e, 0)
                        expert_relu(act, m, e, 1)

                @block.vector
                def _(dve):
                    def weights(g, h, first):
                        b = 2 * g + h
                        window_weights(dve, h, g, first, b, b * SLOTS)
                        window_alpha(dve, h, g)

                    dve.memset(logits[:, :, :], -BIG)
                    for h in range(2):
                        weights(0, h, True)
                        for sub in range(SUBS):
                            window_hot(dve, h, sub)
                        graph_norm(dve, h, 0)
                        graph_features(dve, h, 0)
                    with dve.Fori(1, groups) as g:
                        m = g - 1
                        weights(g, 0, False)
                        for sub in range(SUBS):
                            window_hot(dve, 0, sub)
                        route_top(dve, m)
                        route_probs(dve, m)
                        route_shares(dve, m)
                        bias_residual(dve, m)
                        weights(g, 1, False)
                        window_hot(dve, 1, 0)
                        expert_add(dve, m, 0)
                        graph_norm(dve, 0, g)
                        window_hot(dve, 1, 1)
                        expert_add(dve, m, 1)
                        window_hot(dve, 1, 2)
                        graph_features(dve, 0, g)
                        for e in range(2, EXPERTS - 1):
                            expert_add(dve, m, e)
                        graph_norm(dve, 1, g)
                        expert_add(dve, m, EXPERTS - 1)
                        graph_features(dve, 1, g)
                    m = groups - 1
                    route_top(dve, m)
                    route_probs(dve, m)
                    route_shares(dve, m)
                    bias_residual(dve, m)
                    for e in range(EXPERTS):
                        expert_add(dve, m, e)


def layout(inputs):
    import numpy as np

    def c(v):
        return np.ascontiguousarray(v)

    x, src, dst = inputs["x"], inputs["src"], inputs["dst"]
    padded = -(-x.shape[0] // (2 * P)) * 2 * P
    no_node = np.full(WIN, 1 << 20, dst.dtype)
    arrays = {
        "x": c(np.concatenate([x, np.zeros((padded - x.shape[0], D), x.dtype)])),
        "src": c(np.concatenate([src, np.zeros(WIN, src.dtype)])),
        "dst": c(np.concatenate([dst, no_node])),
        "w_st": c(np.concatenate([inputs["L0_gnn_W_s"].T, inputs["L0_gnn_W_t"].T], axis=1)),
        "w_attn": c(inputs["L0_gnn_W_attn"].reshape(-1)),
        "w_fc": c(inputs["L0_gnn_W_fc"].T),
        "b_fc": c(inputs["L0_gnn_b_fc"]),
        "rw1": c(inputs["L0_ffn_router_w1"]),
        "rb1": c(inputs["L0_ffn_router_b1"].reshape(-1, 1)),
        "rw2": c(inputs["L0_ffn_router_w2"]),
        "rb2": c(inputs["L0_ffn_router_b2"]),
        "ew1": c(inputs["L0_ffn_expert_w1"]),
        "ew2": c(inputs["L0_ffn_expert_w2"]),
        "ew3": c(inputs["L0_ffn_expert_w3"]),
        "eb1": c(inputs["L0_ffn_expert_b1"].reshape(EXPERTS * KD, P).T),
        "eb2": c(inputs["L0_ffn_expert_b2"].reshape(EXPERTS * KD, P).T),
        "eb3": c(inputs["L0_ffn_expert_b3"]),
    }
    return arrays, src.shape[0], padded


def kernel(**inputs):
    import numpy as np
    import concourse.bacc as bacc
    from concourse import mybir as mb
    from concourse.bass_utils import run_bass_kernel_spmd

    arrays, n_edges, padded = layout({k: np.asarray(v) for k, v in inputs.items()})
    nc = bacc.Bacc("TRN2", target_bir_lowering=False, num_devices=1)
    a = {k: nc.dram_tensor("in_" + k, v.shape, mb.dt.from_np(v.dtype), kind="ExternalInput").ap() for k, v in arrays.items()}
    out = nc.dram_tensor("out_x", [padded, D], F32, kind="ExternalOutput").ap()
    a["n_edges"] = n_edges
    gat_moe(nc, a, out)
    r = run_bass_kernel_spmd(nc, [{"in_" + k: v for k, v in arrays.items()}], core_ids=[0])
    return r.results[0]["out_x"][:inputs["x"].shape[0]]
```

```python
from contextlib import ExitStack

import concourse.bass as bass
from concourse import mybir

F32, I32 = mybir.dt.float32, mybir.dt.int32
ALU, ACT, AX = mybir.AluOpType, mybir.ActivationFunctionType, mybir.AxisListType

P = 128
D = 256
KD = D // P
EXPERTS = 6
SLOTS = 18
WIN = P * SLOTS
PAIRS = SLOTS // 2
SUBS = 3
SUB_SLOTS = SLOTS // SUBS
FW = D + 2
PIECE = 64
BIG = 1.0e30
RANGE_MAX = 60.0
EPS = 1e-5
NEG_SLOPE = 0.2


def gat_moe(nc, a, out):
    n_edges, edge_rows = a["n_edges"], 125
    nodes = a["x"].shape[0]
    blocks = nodes // P
    groups = blocks // 2
    windows = blocks * SLOTS
    x_g = a["x"].rearrange("(g h p) c -> g p h c", h=2, p=P)
    out_g = out.rearrange("(g h p) c -> g p h c", h=2, p=P)

    feat = nc.dram_tensor("feat_table", [nodes, FW], F32, kind="Internal").ap()
    ps_table = nc.dram_tensor("ps_table", [nodes, D], F32, kind="Internal").ap()
    ft_table = nc.dram_tensor("ft_table", [nodes, D], F32, kind="Internal").ap()
    pt_table = nc.dram_tensor("pt_table", [nodes, D], F32, kind="Internal").ap()
    starts = nc.dram_tensor("window_starts", [1, blocks], I32, kind="Internal").ap()

    root = ExitStack()

    def tile(name, shape, dt=F32, on=root):
        return on.enter_context(nc.sbuf_tensor(name, shape, dt))

    def bank(name, on, shape=(P, 512)):
        return on.enter_context(nc.psum_tensor(name, list(shape), F32))

    def sem(name, on):
        return on.enter_context(nc.semaphore(name))

    ticks = root.enter_context(nc.semaphore("ticks"))

    def hold(engine, semaphore, value):
        engine.wait_ge(semaphore, value)
        engine.sem_inc(ticks, 1)

    def load_window(engine, start, idx, dst_cols, loaded):
        for to, of in ((idx, a["src"]), (dst_cols, a["dst"])):
            engine.dma_start(to, of[bass.ds(start, WIN)].rearrange("(p k) -> p k", k=SLOTS)).then_inc(loaded, 16)

    with root:
        iota_i = tile("iota_i", [P, P], I32)
        iota = tile("iota", [P, P])
        block_base_i = tile("block_base_i", [P, blocks], I32)
        block_base = tile("block_base", [P, blocks])
        node_id_i = tile("node_id_i", [P, blocks], I32)
        node_id = tile("node_id", [P, blocks])
        ident = tile("ident", [P, P])
        ones = tile("ones", [P, P])
        w_attn = tile("w_attn", [P, D])
        w_sign = tile("w_sign", [P, D])
        b_fc = tile("b_fc", [P, D])
        rb2 = tile("rb2", [P, EXPERTS])
        w_s = tile("w_s", [P, KD, D])
        w_t_fc = tile("w_t_fc", [P, KD, 2 * D])
        rw1 = tile("rw1", [P, KD, P])
        rb1 = tile("rb1", [P, 1])
        rw2 = tile("rw2", [P, EXPERTS])
        ew1 = tile("ew1", [P, EXPERTS * KD, D])
        ew2 = tile("ew2", [P, EXPERTS * KD, D])
        ew3 = tile("ew3", [P, EXPERTS * KD, D])
        eb1 = tile("eb1", [P, EXPERTS * KD])
        eb2 = tile("eb2", [P, EXPERTS * KD])
        eb3 = tile("eb3", [EXPERTS, D])
        e_all = tile("e_all", [P, windows])
        valid_all = tile("valid_all", [P, windows])
        fits = tile("fits", [P, 1], I32)
        shift = tile("shift", [P, 3])

        late_loads = [
            (b_fc[:, :], a["b_fc"].partition_broadcast(P)), (rb2[:, :], a["rb2"].partition_broadcast(P)),
            (rw1[:, :, :], a["rw1"].rearrange("(k p) n -> p k n", p=P)),
            (rb1[:, :], a["rb1"]), (rw2[:, :], a["rw2"]),
            (ew1[:, :, :], a["ew1"].rearrange("e (k p) n -> p (e k) n", p=P)),
            (ew2[:, :, :], a["ew2"].rearrange("e (k p) n -> p (e k) n", p=P)),
            (ew3[:, :, :], a["ew3"].rearrange("e (k p) n -> p (e k) n", p=P)),
            (eb1[:, :], a["eb1"]), (eb2[:, :], a["eb2"]), (eb3[:, :], a["eb3"]),
        ]
        late_weights = sem("late_weights", root)

        per_row = n_edges // edge_rows
        pieces = per_row // PIECE
        with ExitStack() as s:
            dst_rows = tile("dst_rows", [edge_rows, per_row], I32, s)
            last_f = tile("last_f", [edge_rows, pieces], F32, s)
            below = tile("below", [edge_rows, blocks, pieces], F32, s)
            below_sum = tile("below_sum", [edge_rows, blocks], F32, s)
            piece_f = tile("piece_f", [blocks, 1], F32, s)
            piece_i = tile("piece_i", [blocks, 1], I32, s)
            piece_row = tile("piece_row", [blocks, PIECE], I32, s)
            first_node = tile("first_node", [blocks, 1], F32, s)
            inside = tile("inside", [blocks, PIECE], F32, s)
            inside_sum = tile("inside_sum", [blocks, 1], F32, s)
            start_f = tile("start_f", [blocks, 1], F32, s)
            start_i = tile("start_i", [blocks, 1], I32, s)
            first_i = tile("first_i", [P, 1], I32, s)
            piece_count = bank("piece_count", s)
            attn_in, counted, zeroed, base_ok, sign_ok = (sem(n, s) for n in ("attn_in", "counted", "zeroed", "base_ok", "sign_ok"))
            dst_in, last_ok, below_ok, count_ok, piece_ok = (sem(n, s) for n in ("dst_in", "last_ok", "below_ok", "count_ok", "piece_ok"))
            row_in, first_ok, inside_ok, start_ok, stored = (sem(n, s) for n in ("row_in", "first_ok", "inside_ok", "start_ok", "stored"))
            with nc.Block() as block:
                @block.sync
                def _(sp):
                    sp.dma_start(dst_rows[:, :], a["dst"][0:n_edges].rearrange("(p c) -> p c", p=edge_rows)).then_inc(dst_in, 16)
                    sp.dma_start(w_attn[:, :], a["w_attn"].partition_broadcast(P)).then_inc(attn_in, 16)
                    sp.dma_start(w_s[:, :, :], a["w_st"][:, 0:D].rearrange("(k p) n -> p k n", p=P)).then_inc(attn_in, 16)
                    sp.dma_start(w_t_fc[:, :, 0:D], a["w_st"][:, D:2 * D].rearrange("(k p) n -> p k n", p=P)).then_inc(attn_in, 16)
                    sp.dma_start(w_t_fc[:, :, D:2 * D], a["w_fc"].rearrange("(k p) n -> p k n", p=P)).then_inc(attn_in, 16)
                    sp.wait_ge(start_ok, 2)
                    sp.dma_start(starts.rearrange("a b -> b a"), start_i[:, :]).then_inc(stored, 16)
                    sp.wait_ge(stored, 16)

                @block.gpsimd
                def _(gp):
                    gp.iota(block_base_i[:, :], [[P, blocks]], base=0, channel_multiplier=0).then_inc(counted, 1)
                    gp.iota(first_i[:, :], [[0, 1]], base=0, channel_multiplier=P).then_inc(counted, 1)
                    gp.iota(iota_i[:, :], [[1, P]], base=0, channel_multiplier=0).then_inc(counted, 1)
                    gp.iota(node_id_i[:, :], [[P, blocks]], base=0, channel_multiplier=1).then_inc(counted, 1)
                    gp.memset(ones[:, :], 1.0).then_inc(zeroed, 1)
                    gp.memset(ident[:, :], 0.0).then_inc(zeroed, 1)
                    gp.wait_ge(zeroed, 2)
                    gp.affine_select(out=ident[:, :], in_=ident[:, :], compare_op=ALU.not_equal, fill=1.0,
                                     base=0, pattern=[[-1, P]], channel_multiplier=1)
                    gp.wait_ge(piece_ok, 2)
                    gp.indirect_dma_start(piece_row[:, :], None, a["dst"].rearrange("(r c) -> r c", c=PIECE),
                                          bass.IndirectOffsetOnAxis(ap=piece_i[:, :], axis=0)).then_inc(row_in, 16)

                @block.tensor
                def _(pe):
                    pe.wait_ge(zeroed, 1)
                    pe.wait_ge(below_ok, 2)
                    pe.matmul(piece_count[0:blocks, 0:1], below_sum[:, :], ones[0:edge_rows, 0:1],
                              start=True, stop=True).then_inc(count_ok, 1)

                @block.vector
                def _(dve):
                    dve.wait_ge(counted, 4)
                    dve.tensor_copy(block_base[:, :], block_base_i[:, :]).then_inc(base_ok, 1)
                    dve.tensor_copy(first_node[:, :], first_i[0:blocks, :]).then_inc(first_ok, 1)
                    dve.tensor_copy(iota[:, :], iota_i[:, :])
                    dve.tensor_copy(node_id[:, :], node_id_i[:, :])
                    dve.wait_ge(dst_in, 16)
                    dve.tensor_copy(last_f[:, :], dst_rows[:, PIECE - 1::PIECE]).then_inc(last_ok, 1)
                    dve.wait_ge(last_ok, 1)
                    dve.wait_ge(base_ok, 1)
                    dve.tensor_tensor(below[:, :, :], last_f[:, :].unsqueeze(1).to_broadcast([edge_rows, blocks, pieces]),
                                      block_base[0:edge_rows, :].unsqueeze(2).to_broadcast([edge_rows, blocks, pieces]),
                                      ALU.is_lt).then_inc(below_ok, 1)
                    dve.wait_ge(below_ok, 1)
                    dve.tensor_reduce(below_sum[:, :], below[:, :, :], AX.X, ALU.add).then_inc(below_ok, 1)
                    dve.wait_ge(count_ok, 1)
                    dve.tensor_copy(piece_f[:, :], piece_count[0:blocks, 0:1]).then_inc(piece_ok, 1)
                    dve.wait_ge(piece_ok, 1)
                    dve.tensor_copy(piece_i[:, :], piece_f[:, :]).then_inc(piece_ok, 1)
                    dve.wait_ge(attn_in, 64)
                    dve.tensor_scalar(w_sign[:, :], w_attn[:, :], 0.0, 2.0, ALU.is_ge, ALU.mult).then_inc(sign_ok, 1)
                    for w_part in (w_s[:, :, :], w_t_fc[:, :, 0:D]):
                        dve.tensor_tensor(w_part, w_part, w_attn[:, :].unsqueeze(1).to_broadcast([P, KD, D]), ALU.mult)
                    dve.wait_ge(sign_ok, 1)
                    dve.tensor_scalar(w_sign[:, :], w_sign[:, :], -1.0, None, ALU.add)
                    dve.wait_ge(first_ok, 1)
                    dve.wait_ge(row_in, 16)
                    dve.tensor_scalar(inside[:, :], piece_row[:, :], first_node[:, :], None, ALU.is_lt).then_inc(inside_ok, 1)
                    dve.wait_ge(inside_ok, 1)
                    dve.tensor_reduce(inside_sum[:, :], inside[:, :], AX.X, ALU.add).then_inc(inside_ok, 1)
                    dve.wait_ge(inside_ok, 2)
                    dve.scalar_tensor_tensor(start_f[:, :], piece_f[:, :], float(PIECE), inside_sum[:, :],
                                             ALU.mult, ALU.add).then_inc(start_ok, 1)
                    dve.wait_ge(start_ok, 1)
                    dve.tensor_copy(start_i[:, :], start_f[:, :]).then_inc(start_ok, 1)

        lanes = max(n for n in range(1, 8) if blocks % n == 0)
        rounds = blocks // lanes
        banks = 4
        ROOT_AT = lanes - 2
        with ExitStack() as s:
            x_in = [tile(f"x_in{l}", [P, D], F32, s) for l in range(lanes)]
            f = [tile(f"f{l}", [P, D], F32, s) for l in range(lanes)]
            f_t = [tile(f"f_t{l}", [P, KD, P], F32, s) for l in range(lanes)]
            proj = [tile(f"proj{l}", [P, D], F32, s) for l in range(lanes)]
            stats = tile("stats", [P, lanes, 6], F32, s)
            moments = tile("moments", [P, lanes, 2], F32, s)
            std = tile("std", [P, lanes, 1], F32, s)
            rstd = tile("rstd", [P, lanes, 1], F32, s)
            turned = [bank(f"turned{l}", s) for l in range(banks)]
            product = [bank(f"product{l}", s) for l in range(banks)]
            x_loaded = [sem(f"x_loaded{l}", s) for l in range(lanes)]
            proj_stored = [sem(f"proj_stored{l}", s) for l in range(lanes)]
            stats_ok, moments_ok, var_ok, std_ok, rstd_ok, f_ok, turned_ok, ft_ok, product_ok, proj_ok = (
                sem("p_" + n, s) for n in ("stats", "moments", "var", "std", "rstd", "f", "turned", "ft", "product", "proj"))

            def rows_of(table, r, l):
                return table[bass.ds((r * lanes + l) * P, P), :]

            def bank_free(l):
                return banks if l >= banks else min(lanes + l - m for m in range(lanes) if m % banks == l % banks)

            with nc.Block() as block:
                @block.sync
                def _(sp):
                    def step(r, more):
                        for l in range(lanes if more else 0):
                            sp.wait_ge(f_ok, r * lanes + l + 1)
                            sp.dma_start(x_in[l][:, :], rows_of(a["x"], r + 1, l)).then_inc(x_loaded[l], 16)
                        for l in range(lanes):
                            sp.wait_ge(ft_ok, r * lanes + l + 1)
                            sp.dma_start(rows_of(ft_table, r, l), f_t[l][:, :, :]).then_inc(proj_stored[l], 16)
                    for l in range(lanes):
                        sp.dma_start(x_in[l][:, :], rows_of(a["x"], 0, l)).then_inc(x_loaded[l], 16)
                    with sp.Fori(0, rounds - 1) as r:
                        step(r, True)
                    step(rounds - 1, False)

                @block.vector
                def _(dve):
                    def step(r, first):
                        for l in range(lanes):
                            dve.wait_ge(x_loaded[l], 16 * (r + 1))
                            last = dve.bn_stats(stats[:, l, :], x_in[l][:, :])
                        last.then_inc(stats_ok, 1)
                        hold(dve, stats_ok, r + 1)
                        for l in range(lanes):
                            last = dve.bn_aggr(moments[:, l, :], stats[:, l, :])
                        last.then_inc(moments_ok, 1)
                        dve.wait_ge(moments_ok, r + 1)
                        dve.tensor_scalar(std[:, :, :], moments[:, :, 1:2], EPS, None, ALU.add).then_inc(var_ok, 1)
                        dve.wait_ge(std_ok, r + 1)
                        dve.reciprocal(rstd[:, :, :], std[:, :, :]).then_inc(rstd_ok, 1)
                        dve.wait_ge(rstd_ok, r + 1)
                        for l in range(lanes):
                            if not first:
                                dve.wait_ge(turned_ok, (r - 1) * lanes + l + 1)
                            dve.tensor_scalar(f[l][:, :], x_in[l][:, :], moments[:, l, 0:1], rstd[:, l, :],
                                              ALU.subtract, ALU.mult).then_inc(f_ok, 1)
                    step(0, True)
                    with dve.Fori(1, rounds) as r:
                        step(r, False)

                @block.tensor
                def _(pe):
                    def turn(r, l, first):
                        n = r * lanes + l
                        pe.wait_ge(f_ok, n + 1)
                        if not first or l >= banks:
                            pe.wait_ge(ft_ok, n + 1 - bank_free(l))
                        for k in range(KD):
                            last = pe.transpose(turned[l % banks][:, k * P:(k + 1) * P], f[l][:, k * P:(k + 1) * P], ident[:, :])
                        last.then_inc(turned_ok, 1)

                    def project(r, l, first):
                        n = r * lanes + l
                        pe.wait_ge(ft_ok, n + 1)
                        if not first or l >= banks:
                            pe.wait_ge(proj_ok, n + 1 - bank_free(l))
                        for k in range(KD):
                            last = pe.matmul(product[l % banks][:, 0:D], f_t[l][:, k, :], w_s[:, k, :], start=k == 0, stop=k == KD - 1)
                        last.then_inc(product_ok, 1)

                    def step(r, first):
                        turn(r, 0, first)
                        for l in range(1, lanes):
                            turn(r, l, first)
                            project(r, l - 1, first)
                        project(r, lanes - 1, first)
                    step(0, True)
                    with pe.Fori(1, rounds) as r:
                        step(r, False)

                @block.scalar
                def _(act):
                    def copy_turned(r, l, first):
                        act.wait_ge(turned_ok, r * lanes + l + 1)
                        if not first:
                            act.wait_ge(proj_stored[l], 32 * r)
                        act.activation(f_t[l][:, :, :], turned[l % banks][:, 0:D].rearrange("p (k n) -> p k n", k=KD), ACT.Copy).then_inc(ft_ok, 1)

                    def copy_product(r, l):
                        act.wait_ge(product_ok, r * lanes + l + 1)
                        act.activation(proj[l][:, :], product[l % banks][:, 0:D], ACT.Copy).then_inc(proj_ok, 1)
                        act.wait_ge(proj_ok, r * lanes + l + 1)
                        act.dma_start(rows_of(ps_table, r, l), proj[l][:, :]).then_inc(proj_stored[l], 16)

                    def root(r):
                        act.wait_ge(var_ok, r + 1)
                        act.activation(std[:, :, :], std[:, :, :], ACT.Sqrt).then_inc(std_ok, 1)

                    def step(r, first, more):
                        copy_turned(r, 0, first)
                        for l in range(1, lanes):
                            copy_turned(r, l, first)
                            copy_product(r, l - 1)
                            if more and l == ROOT_AT:
                                root(r + 1)
                        copy_product(r, lanes - 1)
                    root(0)
                    step(0, True, True)
                    with act.Fori(1, rounds - 1) as r:
                        step(r, False, True)
                    step(rounds - 1, False, False)
                    for l in range(lanes):
                        act.wait_ge(proj_stored[l], 32 * rounds)

        node_terms = tile("node_terms", [P, blocks, 2])
        pair_ring, z_ring = 6, 6
        HOT_FROM, HOT_SLOTS = 3, 3
        OPEN_AT = 6

        def adds_on_dve(q):
            return q % 3 == 2

        assert (PAIRS - HOT_FROM) * HOT_SLOTS == SLOTS and OPEN_AT + 3 == PAIRS
        with ExitStack() as s:
            idx = [tile(f"sc_idx{h}", [P, SLOTS], I32, s) for h in range(2)]
            dst_cols = [tile(f"sc_dst{h}", [P, SLOTS], I32, s) for h in range(2)]
            dst_row = [tile(f"sc_dst_row{h}", [P, WIN], I32, s) for h in range(2)]
            ft_block = [tile(f"ft_block{h}", [P, KD, P], F32, s) for h in range(2)]
            pt_out_block = [tile(f"pt_out_block{h}", [P, 2 * D], F32, s) for h in range(2)]
            one_hot = [tile(f"one_hot{h}", [P, WIN], F32, s) for h in range(2)]
            local = [tile(f"local{h}", [P, SLOTS], F32, s) for h in range(2)]
            at_least = [tile(f"at_least{h}", [P, SLOTS], F32, s) for h in range(2)]
            gap = [tile(f"sc_gap{h}", [P, SLOTS], F32, s) for h in range(2)]
            src_part = [tile(f"src_part{h}", [P, 2, SLOTS], I32, s) for h in range(2)]
            src_pos = [tile(f"src_pos{h}", [P, 2, SLOTS], F32, s) for h in range(2)]
            weight = [tile(f"weight{h}", [P, SLOTS], F32, s) for h in range(2)]
            lo_hot = [tile(f"lo_hot{h}", [P, SLOTS, P], F32, s) for h in range(2)]
            hi_hot = [tile(f"hi_hot{h}", [P, SLOTS, blocks], F32, s) for h in range(2)]
            ps_rows = [tile(f"ps_rows{r}", [P, 2, D], F32, s) for r in range(pair_ring)]
            z = [tile(f"z{r}", [P, 2, D], F32, s) for r in range(z_ring)]
            unused = [tile(f"unused{r}", [P, 2, D], F32, s) for r in range(z_ring)]
            plain = tile("plain", [P, windows], F32, s)
            first_most = tile("first_most", [P, 1], F32, s)
            first_row = tile("first_row", [1, 1], F32, s)
            taken_off = tile("taken_off", [P, 1], F32, s)
            pt_rows = [bank(f"pt_rows{r}", s) for r in range(z_ring)]
            node_sums = bank("node_sums", s)
            block_bank = bank("block_bank", s)
            loaded = [sem(f"sc_loaded{h}", s) for h in range(2)]
            gathered = [sem(f"sc_gathered{r}", s) for r in range(pair_ring)]
            local_ok, least_ok, one_hot_ok, pt_ok, sum_ok, abs_ok, dot_ok, valid_ok = (
                sem("sc_" + n, s) for n in ("local", "least", "one_hot", "pt", "sum", "abs", "dot", "valid"))
            part_ok, pos_ok, whole_ok, kept_ok, score_ok, exp_ok, hi_hot_ok, lo_hot_ok, added, taken_ok = (
                sem("sc_" + n, s) for n in ("part", "pos", "whole", "kept", "score", "exp", "hi_hot", "lo_hot", "added", "taken"))
            less_ok, weighed_ok, block_ok, block_kept = (sem("sc_" + n, s) for n in ("less", "weighed", "block", "block_kept"))
            block_stored = [sem(f"sc_block_stored{h}", s) for h in range(2)]
            first_ok, first_turned, first_row_ok, first_spread = (
                sem("sc_" + n, s) for n in ("first", "first_turned", "first_row", "first_spread"))

            with nc.Block() as block:
                @block.sync
                def _(sp):
                    def step(g, first):
                        for h in range(2):
                            b = 2 * g + h
                            start = sp.value_load(starts[0:1, bass.ds(b, 1)], min_val=0, max_val=n_edges)
                            if not first:
                                hold(sp, dot_ok, 2 * PAIRS * g + PAIRS * (h - 1))
                                hold(sp, part_ok, 2 * (b - 1))
                            load_window(sp, start, idx[h][:, :], dst_cols[h][:, :], loaded[h])
                            sp.dma_start(dst_row[h][:, :], a["dst"][bass.ds(start, WIN)].partition_broadcast(P)).then_inc(loaded[h], 16)
                            sp.dma_start(ft_block[h][:, :, :], ft_table[bass.ds(b * P, P), :]).then_inc(loaded[h], 16)
                    step(0, True)
                    with sp.Fori(1, groups) as g:
                        step(g, False)
                    sp.wait_ge(dot_ok, PAIRS * blocks)
                    for to, of in late_loads:
                        sp.dma_start(to, of).then_inc(late_weights, 16)

                @block.gpsimd
                def _(gp):
                    def step(g, first):
                        for q in range(2 * PAIRS):
                            h, r, n = q // PAIRS, q % pair_ring, 2 * PAIRS * g + q
                            if q % PAIRS == 0:
                                hold(gp, loaded[h], 64 * (g + 1))
                            if not first or q >= pair_ring:
                                before = (q - pair_ring) % (2 * PAIRS)
                                if adds_on_dve(before):
                                    hold(gp, sum_ok, (n - pair_ring - 2) // 3 + 1 if first else
                                         2 * PAIRS // 3 * g + (q - pair_ring - 2) // 3 + 1)
                                else:
                                    hold(gp, pt_ok, n - pair_ring + 1)
                            for j in range(2):
                                k = 2 * (q % PAIRS) + j
                                gp.indirect_dma_start(ps_rows[r][:, j, :], None, ps_table,
                                                      bass.IndirectOffsetOnAxis(ap=idx[h][:, k:k + 1], axis=0)).then_inc(gathered[r], 16)
                    step(0, True)
                    with gp.Fori(1, groups) as g:
                        step(g, False)

                @block.tensor
                def _(pe):
                    def add_exps(b, h, slots):
                        if slots[0] == 0:
                            pe.wait_ge(lo_hot_ok, 3 * (b + 1))
                            pe.wait_ge(weighed_ok, b + 1)
                        for k in slots:
                            ends = isinstance(b, int)
                            last = pe.matmul(node_sums[:, 0:blocks], lo_hot[h][:, k, :], hi_hot[h][:, k, :],
                                             start=ends and b == 0 and k == 0, stop=ends and b == blocks - 1 and k == SLOTS - 1,
                                             skip_group_check=True)
                        if slots[-1] == SLOTS - 1:
                            last.then_inc(added, 1)

                    def block_product(g, h):
                        b = 2 * g + h
                        pe.wait_ge(loaded[h], 64 * (g + 1))
                        if not (isinstance(b, int) and b == 0):
                            pe.wait_ge(block_kept, b)
                        for k in range(KD):
                            last = pe.matmul(block_bank[:, :], ft_block[h][:, k, :], w_t_fc[:, k, :], start=k == 0, stop=k == KD - 1)
                        last.then_inc(block_ok, 1)

                    def first_maximum():
                        pe.wait_ge(first_ok, 1)
                        pe.transpose(block_bank[0:1, 0:P], first_most[:, :], ident[:, :]).then_inc(first_turned, 1)
                        pe.wait_ge(first_row_ok, 1)
                        pe.matmul(block_bank[:, P:P + 1], ones[0:1, :], first_row[:, :], start=True, stop=True).then_inc(first_spread, 1)

                    def step(g, first, more=True):
                        for q in range(2 * PAIRS):
                            h, r, n = q // PAIRS, q % z_ring, 2 * PAIRS * g + q
                            if q % PAIRS == 0:
                                pe.wait_ge(one_hot_ok, 2 * (2 * g + h + 1))
                                pe.wait_ge(block_kept, 2 * g + h + 1)
                            if not first or q >= z_ring:
                                pe.wait_ge(dot_ok, n - z_ring + 1)
                            on_pe = not adds_on_dve(q)
                            for j in range(2):
                                k = 2 * (q % PAIRS) + j
                                last = pe.matmul(pt_rows[r][:, j * D:(j + 1) * D], one_hot[h][:, k::SLOTS], pt_out_block[h][:, 0:D],
                                                 start=True, stop=not on_pe)
                                if on_pe:
                                    if j == 0:
                                        pe.wait_ge(gathered[q % pair_ring], 32 * (2 * PAIRS // pair_ring * g + q // pair_ring + 1))
                                    last = pe.matmul(pt_rows[r][:, j * D:(j + 1) * D], ident[:, :], ps_rows[q % pair_ring][:, j, :],
                                                     start=False, stop=True)
                            last.then_inc(pt_ok, 1)
                            if first and q == PAIRS + 2:
                                first_maximum()
                            if q % PAIRS == OPEN_AT and (more or h == 0):
                                if first and h == 1:
                                    pe.wait_ge(taken_ok, 1)
                                block_product(g + h, 1 - h)
                            if not first and q % PAIRS >= HOT_FROM:
                                k = (q % PAIRS - HOT_FROM) * HOT_SLOTS
                                add_exps(2 * g + h - 2, h, range(k, k + HOT_SLOTS))
                    block_product(0, 0)
                    step(0, True)
                    step(1, False)
                    with pe.Fori(2, groups - 1) as g:
                        step(g, False)
                    step(groups - 1, False, False)
                    for h in range(2):
                        add_exps(blocks - 2 + h, h, range(SLOTS))

                @block.scalar
                def _(act):
                    def exps(b, h):
                        act.wait_ge(less_ok, b + 1)
                        act.activation(weight[h][:, :], weight[h][:, :], ACT.Exp).then_inc(exp_ok, 1)

                    def weigh_rows(b, h, slots):
                        if slots[0] == 0:
                            act.wait_ge(exp_ok, b + 1)
                            act.wait_ge(hi_hot_ok, b + 1)
                        for k in slots:
                            last = act.activation(hi_hot[h][:, k, :], hi_hot[h][:, k, :], ACT.Copy, scale=weight[h][:, k:k + 1])
                        if slots[-1] == SLOTS - 1:
                            last.then_inc(weighed_ok, 1)

                    def block_keep(g, h, first):
                        b = 2 * g + h
                        act.wait_ge(block_ok, b + 1)
                        if not first:
                            act.wait_ge(block_stored[h], 32 * g)
                        act.activation(pt_out_block[h][:, :], block_bank[:, :], ACT.Copy).then_inc(block_kept, 1)
                        act.wait_ge(block_kept, b + 1)
                        act.dma_start(pt_table[bass.ds(b * P, P), :], pt_out_block[h][:, 0:D]).then_inc(block_stored[h], 16)
                        act.dma_start(feat[bass.ds(b * P, P), 0:D], pt_out_block[h][:, D:2 * D]).then_inc(block_stored[h], 16)

                    def step(g, first, more=True):
                        for q in range(2 * PAIRS):
                            h, r, n = q // PAIRS, q % z_ring, 2 * PAIRS * g + q
                            if q % PAIRS == OPEN_AT + 1 and (more or h == 0):
                                block_keep(g + h, 1 - h, first and h == 0)
                            if adds_on_dve(q):
                                act.wait_ge(sum_ok, 2 * PAIRS // 3 * g + q // 3 + 1)
                                act.activation(z[r][:, :, :], z[r][:, :, :], ACT.Abs).then_inc(abs_ok, 1)
                            else:
                                act.wait_ge(pt_ok, n + 1)
                                for j in range(2):
                                    act.activation(unused[r][:, j, :], pt_rows[r][:, j * D:(j + 1) * D], ACT.Copy,
                                                   accum_out=plain[:, bass.ds(2 * n + j, 1)])
                                act.activation(z[r][:, :, :], pt_rows[r][:, :].rearrange("p (j c) -> p j c", j=2), ACT.Abs).then_inc(abs_ok, 1)
                            if not (first and h == 0):
                                b = 2 * g + h - 1
                                if q % PAIRS == 2:
                                    exps(b, 1 - h)
                                if q % PAIRS >= HOT_FROM:
                                    k = (q % PAIRS - HOT_FROM) * HOT_SLOTS
                                    weigh_rows(b, 1 - h, range(k, k + HOT_SLOTS))
                    block_keep(0, 0, True)
                    step(0, True)
                    with act.Fori(1, groups - 1) as g:
                        step(g, False)
                    step(groups - 1, False, False)
                    for h in range(2):
                        act.wait_ge(block_stored[h], 32 * groups)
                    exps(blocks - 1, 1)
                    weigh_rows(blocks - 1, 1, range(SLOTS))

                @block.vector
                def _(dve):
                    def dot(n, r):
                        dve.wait_ge(abs_ok, n + 1)
                        for j in range(2):
                            last = dve.scalar_tensor_tensor(z[r][:, j, :], z[r][:, j, :], (1 - NEG_SLOPE) / 2, w_sign[:, :],
                                                            ALU.mult, ALU.mult, accum_out=e_all[:, bass.ds(2 * n + j, 1)])
                        last.then_inc(dot_ok, 1)

                    def open_block(g, h):
                        b = 2 * g + h
                        dve.wait_ge(loaded[h], 64 * (g + 1))
                        dve.tensor_scalar(local[h][:, :], dst_cols[h][:, :], block_base[:, bass.ds(b, 1)], None,
                                          ALU.subtract).then_inc(local_ok, 1)
                        dve.tensor_scalar(src_part[h][:, 0, :], idx[h][:, :], 7, None, ALU.logical_shift_right).then_inc(part_ok, 1)
                        dve.tensor_scalar(src_part[h][:, 1, :], idx[h][:, :], P - 1, None, ALU.bitwise_and).then_inc(part_ok, 1)
                        dve.wait_ge(local_ok, b + 1)
                        dve.tensor_scalar(at_least[h][:, :], local[h][:, :], 0.0, None, ALU.is_ge).then_inc(least_ok, 1)
                        dve.wait_ge(part_ok, 2 * b + 2)
                        dve.tensor_copy(src_pos[h][:, :, :], src_part[h][:, :, :]).then_inc(pos_ok, 1)
                        dve.wait_ge(least_ok, b + 1)
                        dve.scalar_tensor_tensor(valid_all[:, bass.ds(b * SLOTS, SLOTS)], local[h][:, :], float(P),
                                                 at_least[h][:, :], ALU.is_lt, ALU.mult).then_inc(valid_ok, 1)
                        dve.wait_ge(valid_ok, b + 1)
                        dve.tensor_scalar(gap[h][:, :], valid_all[:, bass.ds(b * SLOTS, SLOTS)], BIG, -BIG, ALU.mult, ALU.add)

                    def one_hot_half(g, h, half):
                        cols = slice(half * WIN // 2, (half + 1) * WIN // 2)
                        dve.tensor_scalar(one_hot[h][:, cols], dst_row[h][:, cols], node_id[:, bass.ds(2 * g + h, 1)], None,
                                          ALU.is_equal).then_inc(one_hot_ok, 1)

                    def score(b, h):
                        cols = bass.ds(b * SLOTS, SLOTS)
                        dve.wait_ge(dot_ok, PAIRS * (b + 1))
                        dve.scalar_tensor_tensor(e_all[:, cols], plain[:, cols], (1 + NEG_SLOPE) / 2, e_all[:, cols],
                                                 ALU.mult, ALU.add).then_inc(whole_ok, 1)
                        dve.wait_ge(whole_ok, b + 1)
                        dve.tensor_tensor(e_all[:, cols], e_all[:, cols], valid_all[:, cols], ALU.mult).then_inc(kept_ok, 1)
                        dve.wait_ge(kept_ok, b + 1)
                        dve.tensor_tensor(e_all[:, cols], e_all[:, cols], gap[h][:, :], ALU.add).then_inc(score_ok, 1)

                    def hi_rows(b, h, first):
                        dve.wait_ge(pos_ok, b + 1)
                        if not first:
                            dve.wait_ge(added, b - 1)
                        dve.tensor_tensor(hi_hot[h][:, :, :], src_pos[h][:, 0, :].unsqueeze(2).to_broadcast([P, SLOTS, blocks]),
                                          iota[:, 0:blocks].unsqueeze(1).to_broadcast([P, SLOTS, blocks]),
                                          ALU.is_equal).then_inc(hi_hot_ok, 1)

                    def less(b, h):
                        dve.wait_ge(taken_ok, 1)
                        dve.wait_ge(score_ok, b + 1)
                        dve.tensor_scalar(weight[h][:, :], e_all[:, bass.ds(b * SLOTS, SLOTS)], taken_off[:, :], RANGE_MAX,
                                          ALU.subtract, ALU.min).then_inc(less_ok, 1)

                    def lo_rows(h, third):
                        some = slice(third * SLOTS // 3, (third + 1) * SLOTS // 3)
                        dve.tensor_tensor(lo_hot[h][:, some, :], src_pos[h][:, 1, some].unsqueeze(2).to_broadcast([P, SLOTS // 3, P]),
                                          iota[:, :].unsqueeze(1).to_broadcast([P, SLOTS // 3, P]), ALU.is_equal).then_inc(lo_hot_ok, 1)

                    def first_maximum():
                        dve.wait_ge(score_ok, 1)
                        dve.tensor_reduce(first_most[:, :], e_all[:, 0:SLOTS], AX.X, ALU.max).then_inc(first_ok, 1)
                        dve.wait_ge(first_turned, 1)
                        dve.tensor_reduce(first_row[:, :], block_bank[0:1, 0:P], AX.X, ALU.max).then_inc(first_row_ok, 1)
                        dve.wait_ge(first_spread, 1)
                        dve.tensor_copy(taken_off[:, :], block_bank[:, P:P + 1]).then_inc(taken_ok, 1)

                    def step(g, first, more=True):
                        for q in range(2 * PAIRS):
                            h, r, n = q // PAIRS, q % z_ring, 2 * PAIRS * g + q
                            before = not (first and h == 0)
                            if q % PAIRS >= OPEN_AT and (more or h == 0):
                                if q % PAIRS == OPEN_AT:
                                    open_block(g + h, 1 - h)
                                else:
                                    one_hot_half(g + h, 1 - h, q % PAIRS - OPEN_AT - 1)
                            if adds_on_dve(q):
                                dve.wait_ge(gathered[q % pair_ring], 32 * (2 * PAIRS // pair_ring * g + q // pair_ring + 1))
                                dve.wait_ge(pt_ok, n + 1)
                                for j in range(2):
                                    last = dve.scalar_tensor_tensor(z[r][:, j, :], ps_rows[q % pair_ring][:, j, :], 1.0,
                                                                    pt_rows[r][:, j * D:(j + 1) * D], ALU.mult, ALU.add,
                                                                    accum_out=plain[:, bass.ds(2 * n + j, 1)])
                                last.then_inc(sum_ok, 1)
                            if not first or q >= 2:
                                dot(n - 2, (q - 2) % z_ring)
                            b = 2 * g + h - 1
                            if q % PAIRS == 1 and before:
                                score(b, 1 - h)
                                if first:
                                    first_maximum()
                            if q % PAIRS == 2 and before:
                                hi_rows(b, 1 - h, first or (isinstance(g, int) and g == 1 and h == 0))
                                less(b, 1 - h)
                            if q % PAIRS in (3, 4, 5) and before:
                                lo_rows(1 - h, q % PAIRS - 3)
                    open_block(0, 0)
                    for half in range(2):
                        one_hot_half(0, 0, half)
                    step(0, True)
                    step(1, False)
                    with dve.Fori(2, groups - 1) as g:
                        step(g, False)
                    step(groups - 1, False, False)
                    for n in (groups * 2 * PAIRS - 2, groups * 2 * PAIRS - 1):
                        dot(n, n % z_ring)
                    score(blocks - 1, 1)
                    hi_rows(blocks - 1, 1, False)
                    less(blocks - 1, 1)
                    for third in range(3):
                        lo_rows(1, third)

            masked = lo_hot[0][:, :, :].rearrange("p k n -> p (k n)")[:, 0:windows]
            extreme = at_least[0]
            turned_sb = tile("turned_sb", [1, 2], F32, s)
            verdict = tile("verdict", [P, 8], F32, s)
            rescale = tile("rescale", [P, 2], F32, s)
            total = tile("total", [P, blocks], F32, s)
            step_ok, found_ok, turned_ok, row_ok, spread_ok, off_ok, scale_ok, terms_ok, stored = (
                sem("j_" + n, s) for n in ("step", "found", "turned", "row", "spread", "off", "scale", "terms", "stored"))
            with nc.Block() as block:
                @block.vector
                def _(dve):
                    dve.tensor_tensor(masked, e_all[:, :], valid_all[:, :], ALU.mult).then_inc(step_ok, 1)
                    dve.tensor_scalar(plain[:, :], valid_all[:, :], BIG, -BIG, ALU.mult, ALU.add).then_inc(step_ok, 1)
                    dve.tensor_reduce(extreme[:, 2:3], valid_all[:, :], AX.X, ALU.add)
                    dve.tensor_reduce(extreme[:, 0:1], e_all[:, :], AX.X, ALU.max).then_inc(found_ok, 1)
                    dve.wait_ge(step_ok, 2)
                    dve.tensor_tensor(masked, plain[:, :], masked, ALU.subtract).then_inc(step_ok, 1)
                    dve.wait_ge(step_ok, 3)
                    dve.tensor_reduce(extreme[:, 1:2], masked, AX.X, ALU.max).then_inc(found_ok, 1)
                    dve.wait_ge(turned_ok, 1)
                    dve.tensor_reduce(turned_sb[:, :], pt_rows[0][0:1, 0:2 * P].rearrange("a (m n) -> a m n", m=2),
                                      AX.X, ALU.max).then_inc(row_ok, 1)
                    dve.wait_ge(spread_ok, 1)
                    dve.tensor_copy(shift[:, :], pt_rows[1][:, 0:3]).then_inc(step_ok, 1)
                    dve.wait_ge(step_ok, 4)
                    dve.tensor_tensor(rescale[:, 0:1], taken_off[:, :], shift[:, 0:1], ALU.subtract).then_inc(off_ok, 1)
                    dve.tensor_tensor(verdict[:, 0:1], shift[:, 0:1], shift[:, 1:2], ALU.add).then_inc(step_ok, 1)
                    dve.tensor_scalar(verdict[:, 1:2], shift[:, 2:3], float(n_edges), None, ALU.is_equal).then_inc(step_ok, 1)
                    dve.wait_ge(off_ok, 1)
                    dve.tensor_scalar(verdict[:, 2:3], rescale[:, 0:1], -RANGE_MAX, None, ALU.is_ge).then_inc(step_ok, 1)
                    dve.wait_ge(step_ok, 7)
                    dve.scalar_tensor_tensor(verdict[:, 3:4], verdict[:, 0:1], RANGE_MAX, verdict[:, 1:2],
                                             ALU.is_le, ALU.mult).then_inc(step_ok, 1)
                    dve.wait_ge(step_ok, 8)
                    dve.tensor_tensor(verdict[:, 4:5], verdict[:, 3:4], verdict[:, 2:3], ALU.mult).then_inc(step_ok, 1)
                    dve.wait_ge(step_ok, 9)
                    dve.tensor_copy(fits[:, :], verdict[:, 4:5])
                    dve.wait_ge(scale_ok, 1)
                    dve.tensor_scalar(total[:, :], node_sums[:, 0:blocks], rescale[:, 1:2], 1e-37, ALU.mult, ALU.max).then_inc(step_ok, 1)
                    dve.wait_ge(step_ok, 10)
                    dve.reciprocal(node_terms[:, :, 1:2], total[:, :].unsqueeze(2)).then_inc(terms_ok, 1)
                    dve.tensor_copy(node_terms[:, :, 0:1], shift[:, 0:1].unsqueeze(1).to_broadcast([P, blocks, 1])).then_inc(terms_ok, 1)

                @block.scalar
                def _(act):
                    act.wait_ge(off_ok, 1)
                    act.activation(rescale[:, 1:2], rescale[:, 0:1], ACT.Exp).then_inc(scale_ok, 1)

                @block.sync
                def _(sp):
                    sp.wait_ge(terms_ok, 2)
                    sp.dma_start(feat[:, D:D + 2].rearrange("(b p) c -> p b c", p=P), node_terms[:, :, :]).then_inc(stored, 16)
                    sp.wait_ge(stored, 16)
                    sp.wait_ge(late_weights, 16 * len(late_loads))

                @block.tensor
                def _(pe):
                    pe.wait_ge(found_ok, 2)
                    for m in range(2):
                        last = pe.transpose(pt_rows[0][0:1, m * P:(m + 1) * P], extreme[:, m:m + 1], ident[:, :])
                    last.then_inc(turned_ok, 1)
                    pe.matmul(pt_rows[1][:, 2:3], ones[:, :], extreme[:, 2:3], start=True, stop=True)
                    pe.wait_ge(row_ok, 1)
                    pe.matmul(pt_rows[1][:, 0:2], ones[0:1, :], turned_sb[:, :], start=True, stop=True).then_inc(spread_ok, 1)

        all_windows = -(-n_edges // WIN)
        assert all_windows * SLOTS <= windows and (all_windows - 1) * WIN + WIN <= n_edges + WIN
        e_flat = nc.dram_tensor("e_flat", [all_windows * WIN], F32, kind="Internal").ap()
        with ExitStack() as s:
            idx = tile("any_idx", [P, SLOTS], I32, s)
            dst_cols = tile("any_dst", [P, SLOTS], I32, s)
            dst_idx = tile("any_dst_idx", [P, SLOTS], I32, s)
            ps_row = tile("any_ps", [P, D], F32, s)
            pt_row = tile("any_pt", [P, D], F32, s)
            z = tile("any_z", [P, D], F32, s)
            plain = tile("any_plain", [P, windows], F32, s)
            gap = tile("any_gap", [P, windows], F32, s)
            loaded, clamped, gathered, sum_ok, abs_ok, dot_ok, end_ok, stored = (
                sem("any_" + n, s) for n in ("loaded", "clamped", "gathered", "sum", "abs", "dot", "end", "stored"))
            with nc.Block() as block:
                @block.sync
                def _(sp):
                    fit = sp.value_load(fits[0:1, 0:1], min_val=0, max_val=1)
                    with sp.If(fit == 0):
                        with sp.Fori(0, all_windows) as w:
                            hold(sp, dot_ok, SLOTS * (w + 1))
                            load_window(sp, w * WIN, idx[:, :], dst_cols[:, :], loaded)
                        sp.wait_ge(end_ok, 5)
                        sp.dma_start(e_flat.rearrange("(w p k) -> p w k", p=P, k=SLOTS),
                                     e_all[:, 0:all_windows * SLOTS].rearrange("p (w k) -> p w k", k=SLOTS)).then_inc(stored, 16)
                        sp.wait_ge(stored, 16)

                @block.gpsimd
                def _(gp):
                    fit = gp.value_load(fits[0:1, 0:1], min_val=0, max_val=1)
                    with gp.If(fit == 0):
                        with gp.Fori(0, all_windows) as w:
                            hold(gp, loaded, 32 * (w + 1))
                            hold(gp, clamped, w + 2)
                            for k in range(SLOTS):
                                hold(gp, dot_ok, SLOTS * (w + 1) + k)
                                gp.indirect_dma_start(ps_row[:, :], None, ps_table,
                                                      bass.IndirectOffsetOnAxis(ap=idx[:, k:k + 1], axis=0)).then_inc(gathered, 16)
                                gp.indirect_dma_start(pt_row[:, :], None, pt_table,
                                                      bass.IndirectOffsetOnAxis(ap=dst_idx[:, k:k + 1], axis=0)).then_inc(gathered, 16)

                @block.scalar
                def _(act):
                    fit = act.value_load(fits[0:1, 0:1], min_val=0, max_val=1)
                    with act.If(fit == 0):
                        act.sem_inc(abs_ok, SLOTS)
                        with act.Fori(0, all_windows) as w:
                            for k in range(SLOTS):
                                act.wait_ge(sum_ok, SLOTS * (w + 1) + k + 1)
                                act.activation(z[:, :], z[:, :], ACT.Abs).then_inc(abs_ok, 1)

                @block.vector
                def _(dve):
                    fit = dve.value_load(fits[0:1, 0:1], min_val=0, max_val=1)
                    with dve.If(fit == 0):
                        dve.sem_inc(clamped, 1)
                        dve.sem_inc(sum_ok, SLOTS)
                        dve.sem_inc(dot_ok, SLOTS)
                        with dve.Fori(0, all_windows) as w:
                            dve.wait_ge(loaded, 32 * (w + 1))
                            dve.tensor_scalar(valid_all[:, bass.ds(w * SLOTS, SLOTS)], dst_cols[:, :], float(nodes), None, ALU.is_lt)
                            dve.tensor_scalar(dst_idx[:, :], dst_cols[:, :], float(nodes - 1), None, ALU.min).then_inc(clamped, 1)
                            for k in range(SLOTS):
                                dve.wait_ge(gathered, 32 * (SLOTS * w + k + 1))
                                dve.wait_ge(dot_ok, SLOTS * (w + 1) + k)
                                dve.scalar_tensor_tensor(z[:, :], ps_row[:, :], 1.0, pt_row[:, :], ALU.mult, ALU.add,
                                                         accum_out=plain[:, bass.ds(w * SLOTS + k, 1)]).then_inc(sum_ok, 1)
                                dve.wait_ge(abs_ok, SLOTS * (w + 1) + k + 1)
                                dve.scalar_tensor_tensor(z[:, :], z[:, :], (1 - NEG_SLOPE) / 2, w_sign[:, :], ALU.mult, ALU.mult,
                                                         accum_out=e_all[:, bass.ds(w * SLOTS + k, 1)]).then_inc(dot_ok, 1)
                        dve.drain().then_inc(end_ok, 1)
                        dve.wait_ge(end_ok, 1)
                        whole = slice(0, all_windows * SLOTS)
                        dve.scalar_tensor_tensor(e_all[:, whole], plain[:, whole], (1 + NEG_SLOPE) / 2, e_all[:, whole],
                                                 ALU.mult, ALU.add).then_inc(end_ok, 1)
                        dve.tensor_scalar(gap[:, whole], valid_all[:, whole], BIG, -BIG, ALU.mult, ALU.add).then_inc(end_ok, 1)
                        dve.wait_ge(end_ok, 3)
                        dve.tensor_tensor(e_all[:, whole], e_all[:, whole], valid_all[:, whole], ALU.mult).then_inc(end_ok, 1)
                        dve.wait_ge(end_ok, 4)
                        dve.tensor_tensor(e_all[:, whole], e_all[:, whole], gap[:, whole], ALU.add).then_inc(end_ok, 1)

        with ExitStack() as s:
            src_row = tile("any_src_row", [P, WIN], I32, s)
            e_row = tile("any_e_row", [P, WIN], F32, s)
            mine = tile("any_mine", [P, WIN], F32, s)
            gap = tile("any_row_gap", [P, WIN], F32, s)
            part = tile("any_part", [P, 1], F32, s)
            most = tile("any_most", [P, 1], F32, s)
            total = tile("any_total", [P, 1], F32, s)
            loaded, went, exp_in, exp_out, stored = (sem("node_" + n, s) for n in ("loaded", "went", "exp_in", "exp_out", "stored"))
            MAX_STEPS, SUM_STEPS, OPEN_STEPS, CLOSE_STEPS = 6, 5, 2, 3
            BLOCK_STEPS = OPEN_STEPS + all_windows * (MAX_STEPS + SUM_STEPS) + CLOSE_STEPS
            with nc.Block() as block:
                @block.sync
                def _(sp):
                    fit = sp.value_load(fits[0:1, 0:1], min_val=0, max_val=1)
                    with sp.If(fit == 0):
                        def load(w):
                            sp.dma_start(src_row[:, :], a["src"][bass.ds(w * WIN, WIN)].partition_broadcast(P)).then_inc(loaded, 16)
                            sp.dma_start(e_row[:, :], e_flat[bass.ds(w * WIN, WIN)].partition_broadcast(P)).then_inc(loaded, 16)

                        with sp.Fori(0, blocks) as b:
                            with sp.Fori(0, all_windows) as w:
                                hold(sp, went, b * BLOCK_STEPS + OPEN_STEPS + w * MAX_STEPS)
                                load(w)
                            with sp.Fori(0, all_windows) as w:
                                hold(sp, went, b * BLOCK_STEPS + OPEN_STEPS + all_windows * MAX_STEPS + w * SUM_STEPS)
                                load(w)
                        sp.wait_ge(went, blocks * BLOCK_STEPS)
                        sp.dma_start(feat[:, D:D + 2].rearrange("(b p) c -> p b c", p=P), node_terms[:, :, :]).then_inc(stored, 16)
                        sp.wait_ge(stored, 16)

                @block.scalar
                def _(act):
                    fit = act.value_load(fits[0:1, 0:1], min_val=0, max_val=1)
                    with act.If(fit == 0):
                        with act.Fori(0, blocks) as b:
                            with act.Fori(0, all_windows) as w:
                                act.wait_ge(exp_in, b * all_windows + w + 1)
                                act.activation(e_row[:, :], e_row[:, :], ACT.Exp).then_inc(exp_out, 1)

                @block.vector
                def _(dve):
                    fit = dve.value_load(fits[0:1, 0:1], min_val=0, max_val=1)
                    with dve.If(fit == 0):
                        with dve.Fori(0, blocks) as b:
                            base = b * BLOCK_STEPS
                            dve.tensor_scalar(most[:, :], ones[:, 0:1], -BIG, None, ALU.mult).then_inc(went, 1)
                            dve.tensor_scalar(total[:, :], ones[:, 0:1], 0.0, None, ALU.mult).then_inc(went, 1)
                            with dve.Fori(0, all_windows) as w:
                                at = base + OPEN_STEPS + w * MAX_STEPS
                                hold(dve, went, at)
                                dve.wait_ge(loaded, 32 * (b * (2 * all_windows) + w + 1))
                                dve.tensor_scalar(mine[:, :], src_row[:, :], node_id[:, bass.ds(b, 1)], None, ALU.is_equal).then_inc(went, 1)
                                dve.wait_ge(went, at + 1)
                                dve.tensor_scalar(gap[:, :], mine[:, :], BIG, -BIG, ALU.mult, ALU.add).then_inc(went, 1)
                                dve.tensor_tensor(e_row[:, :], e_row[:, :], mine[:, :], ALU.mult).then_inc(went, 1)
                                dve.wait_ge(went, at + 3)
                                dve.tensor_tensor(e_row[:, :], e_row[:, :], gap[:, :], ALU.add).then_inc(went, 1)
                                dve.wait_ge(went, at + 4)
                                dve.tensor_reduce(part[:, :], e_row[:, :], AX.X, ALU.max).then_inc(went, 1)
                                dve.wait_ge(went, at + 5)
                                dve.tensor_tensor(most[:, :], most[:, :], part[:, :], ALU.max).then_inc(went, 1)
                            with dve.Fori(0, all_windows) as w:
                                at = base + OPEN_STEPS + all_windows * MAX_STEPS + w * SUM_STEPS
                                hold(dve, went, at)
                                dve.wait_ge(loaded, 32 * (b * (2 * all_windows) + all_windows + w + 1))
                                dve.tensor_scalar(mine[:, :], src_row[:, :], node_id[:, bass.ds(b, 1)], None, ALU.is_equal).then_inc(went, 1)
                                dve.tensor_scalar(e_row[:, :], e_row[:, :], most[:, :], 0.0, ALU.subtract, ALU.min).then_inc(exp_in, 1)
                                dve.wait_ge(exp_out, b * all_windows + w + 1)
                                dve.wait_ge(went, at + 1)
                                dve.tensor_tensor(e_row[:, :], e_row[:, :], mine[:, :], ALU.mult).then_inc(went, 1)
                                dve.wait_ge(went, at + 2)
                                dve.tensor_reduce(part[:, :], e_row[:, :], AX.X, ALU.add).then_inc(went, 1)
                                dve.wait_ge(went, at + 3)
                                dve.tensor_tensor(total[:, :], total[:, :], part[:, :], ALU.add).then_inc(went, 2)
                            close = base + OPEN_STEPS + all_windows * (MAX_STEPS + SUM_STEPS)
                            dve.wait_ge(went, close)
                            dve.tensor_scalar(total[:, :], total[:, :], 1e-37, None, ALU.max).then_inc(went, 1)
                            dve.wait_ge(went, close + 1)
                            dve.tensor_copy(node_terms[:, bass.ds(b, 1), 0:1], most[:, :].unsqueeze(2)).then_inc(went, 1)
                            dve.reciprocal(node_terms[:, bass.ds(b, 1), 1:2], total[:, :].unsqueeze(2)).then_inc(went, 1)
                            hold(dve, went, close + 3)

        with ExitStack() as s:
            idx = [tile(f"mx_idx{h}", [P, SLOTS], I32, s) for h in range(2)]
            dst_cols = [tile(f"mx_dst{h}", [P, SLOTS], I32, s) for h in range(2)]
            local = [tile(f"mx_local{h}", [P, SLOTS], F32, s) for h in range(2)]
            alpha = [tile(f"alpha{h}", [P, SLOTS], F32, s) for h in range(2)]
            f_rows = [tile(f"f_rows{h}", [P, SLOTS, FW], F32, s) for h in range(2)]
            alpha_hot = [tile(f"alpha_hot{h}", [P, SLOTS, P], F32, s) for h in range(2)]
            agg = [tile(f"agg{h}", [P, D], F32, s) for h in range(2)]
            x_in = tile("mx_x", [P, 2, D], F32, s)
            x1 = [tile(f"x1_{h}", [P, D], F32, s) for h in range(2)]
            f1 = [tile(f"f1_{h}", [P, D], F32, s) for h in range(2)]
            stats = [tile(f"mx_stats{h}", [P, 6], F32, s) for h in range(2)]
            moments = [tile(f"mx_moments{h}", [P, 2], F32, s) for h in range(2)]
            std = [tile(f"mx_std{h}", [P, 1], F32, s) for h in range(2)]
            rstd = [tile(f"mx_rstd{h}", [P, 1], F32, s) for h in range(2)]
            f1_t = tile("f1_t", [P, KD, 2 * P], F32, s)
            rh_t = tile("rh_t", [P, 2 * P], F32, s)
            logits = tile("logits", [P, 2, 8], F32, s)
            top = tile("top", [P, 2, 8], F32, s)
            top_i = tile("top_i", [P, 2, 8], mybir.dt.uint32, s)
            top_f = tile("top_f", [P, 4], F32, s)
            less_top = tile("less_top", [P, 2, 8], F32, s)
            exps = tile("exps", [P, 2, 8], F32, s)
            norm = tile("norm", [P, 2, 2], F32, s)
            pick = tile("pick", [P, 2, 2, 8], F32, s)
            share = tile("share", [P, 2, 8], F32, s)
            share_t = tile("share_t", [8, 2 * P], F32, s)
            h1_t = [tile(f"h1_t{i}", [P, KD, 2 * P], F32, s) for i in range(2)]
            h2_t = [tile(f"h2_t{i}", [P, KD, 2 * P], F32, s) for i in range(2)]
            mixed = tile("mixed", [P, 2, D], F32, s)

            agg_bank = [bank(f"agg_bank{h}", s) for h in range(2)]
            layer_bank = [bank(f"layer_bank{i}", s) for i in range(3)]
            f1_bank = bank("f1_bank", s)
            router_bank = bank("router_bank", s)

            loaded = [sem(f"mx_loaded{h}", s) for h in range(2)]
            gathered = [sem(f"mx_gathered{h}", s) for h in range(2)]
            local_ok, diff_ok, min_ok, exp_ok, alpha_ok, hot_ok, used = (
                [sem(f"mx_{n}{h}", s) for h in range(2)] for n in ("local", "diff", "min", "exp", "alpha", "hot", "used"))
            res_ok, x1_ok, stats_ok, moments_ok, var_ok, std_ok, rstd_ok, f1_ok = (
                [sem(f"mx_{n}{h}", s) for h in range(2)]
                for n in ("res", "x1", "stats", "moments", "var", "std", "rstd", "f1"))
            x_loaded, f1_turned, f1_t_ok, rh_ok, rh_t_ok, logit_ok, share_ok, share_turned, share_t_ok, bias_ok = (
                sem("mx_" + n, s) for n in ("x_loaded", "f1_turned", "f1_t", "rh", "rh_t", "logit", "share",
                                            "share_turned", "share_t", "bias"))
            made_ok = [sem(f"mx_made{i}", s) for i in range(3)]
            kept_ok = [sem(f"mx_kept{i}", s) for i in range(3)]
            out_stored = sem("mx_out_stored", s)
            route = sem("mx_route", s)
            mixed_free = sem("mx_mixed_free", s)
            cleared = sem("mx_cleared", s)
            added = [sem(f"mx_added{h}", s) for h in range(2)]

            def x_rows(table, g):
                return table[bass.ds(g, 1), :, :, :].rearrange("a p h c -> (a p) h c")

            def window_load(sp, start, h, n, first):
                if not first:
                    hold(sp, hot_ok[h], SUBS * n - SUBS + 1)
                load_window(sp, start, idx[h][:, :], dst_cols[h][:, :], loaded[h])

            def window_gather(gp, h, n, first, credit=0):
                hold(gp, loaded[h], 32 * (n + 1 - credit))
                for k in range(SLOTS):
                    if not first and k % SUB_SLOTS == 0:
                        hold(gp, used[h], SUBS * n - SUBS + k // SUB_SLOTS + 1)
                    gp.indirect_dma_start(f_rows[h][:, k, :], None, feat,
                                          bass.IndirectOffsetOnAxis(ap=idx[h][:, k:k + 1], axis=0)).then_inc(gathered[h], 16)

            def window_weights(dve, h, n, first, b, score_at, credit=0):
                dve.wait_ge(loaded[h], 32 * (n + 1 - credit))
                if not first:
                    dve.wait_ge(used[h], SUBS * n)
                dve.tensor_scalar(local[h][:, :], dst_cols[h][:, :], block_base[:, bass.ds(b, 1)], None,
                                  ALU.subtract).then_inc(local_ok[h], 1)
                dve.wait_ge(gathered[h], SLOTS * 16 * (n + 1 - credit))
                dve.tensor_tensor(alpha[h][:, :].unsqueeze(2), e_all[:, bass.ds(score_at, SLOTS)].unsqueeze(2),
                                  f_rows[h][:, :, D:D + 1], ALU.subtract).then_inc(diff_ok[h], 1)
                dve.wait_ge(diff_ok[h], n + 1)
                dve.tensor_scalar(alpha[h][:, :], alpha[h][:, :], 0.0, None, ALU.min).then_inc(min_ok[h], 1)

            def window_exp(act, h, n):
                act.wait_ge(min_ok[h], n + 1)
                act.activation(alpha[h][:, :], alpha[h][:, :], ACT.Exp).then_inc(exp_ok[h], 1)

            def window_alpha(dve, h, n):
                dve.wait_ge(exp_ok[h], n + 1)
                dve.tensor_tensor(alpha[h][:, :].unsqueeze(2), alpha[h][:, :].unsqueeze(2), f_rows[h][:, :, D + 1:D + 2],
                                  ALU.mult).then_inc(alpha_ok[h], 1)
                dve.wait_ge(alpha_ok[h], n + 1)

            def window_hot(dve, h, sub):
                for k in range(sub * SUB_SLOTS, (sub + 1) * SUB_SLOTS):
                    last = dve.tensor_scalar(alpha_hot[h][:, k, :], iota[:, :], local[h][:, k:k + 1], alpha[h][:, k:k + 1],
                                             ALU.is_equal, ALU.mult)
                last.then_inc(hot_ok[h], 1)

            def window_add(pe, h, n, sub, half):
                if half == 0:
                    pe.wait_ge(hot_ok[h], SUBS * n + sub + 1)
                k0 = sub * SUB_SLOTS + half * (SUB_SLOTS // 2)
                for k in range(k0, k0 + SUB_SLOTS // 2):
                    last = pe.matmul(agg_bank[h][:, 0:D], alpha_hot[h][:, k, :], f_rows[h][:, k, 0:D],
                                     start=k == 0, stop=k == SLOTS - 1)
                if half == 1:
                    last.then_inc(used[h], 1)

            def graph_norm(dve, h, g, sums, sums_ok, sums_at, credit=0):
                dve.wait_ge(x_loaded, 16 * (g + 1 - credit))
                dve.tensor_tensor(x1[h][:, :], x_in[:, h, :], b_fc[:, :], ALU.add).then_inc(res_ok[h], 1)
                dve.wait_ge(sums_ok, sums_at)
                dve.wait_ge(res_ok[h], g + 1)
                dve.tensor_tensor(x1[h][:, :], sums, x1[h][:, :], ALU.add).then_inc(x1_ok[h], 1)
                dve.wait_ge(x1_ok[h], g + 1)
                dve.bn_stats(stats[h][:, :], x1[h][:, :]).then_inc(stats_ok[h], 1)
                hold(dve, stats_ok[h], g + 1)
                dve.bn_aggr(moments[h][:, :], stats[h][:, :]).then_inc(moments_ok[h], 1)
                dve.wait_ge(moments_ok[h], g + 1)
                dve.tensor_scalar(std[h][:, :], moments[h][:, 1:2], EPS, None, ALU.add).then_inc(var_ok[h], 1)

            def graph_root(act, h, g):
                act.wait_ge(var_ok[h], g + 1)
                act.activation(std[h][:, :], std[h][:, :], ACT.Sqrt).then_inc(std_ok[h], 1)

            def graph_features(dve, h, g):
                dve.wait_ge(std_ok[h], g + 1)
                dve.reciprocal(rstd[h][:, :], std[h][:, :]).then_inc(rstd_ok[h], 1)
                dve.wait_ge(rstd_ok[h], g + 1)
                dve.tensor_scalar(f1[h][:, :], x1[h][:, :], moments[h][:, 0:1], rstd[h][:, :],
                                  ALU.subtract, ALU.mult).then_inc(f1_ok[h], 1)

            def moe_turn(pe, m):
                for h in (1, 0):
                    pe.wait_ge(f1_ok[h], m + 1)
                    for k in range(KD):
                        last = pe.transpose(f1_bank[:, (2 * k + h) * P:(2 * k + h + 1) * P], f1[h][:, k * P:(k + 1) * P], ident[:, :])
                last.then_inc(f1_turned, 1)

            def moe_turned(act, m):
                act.wait_ge(f1_turned, m + 1)
                act.activation(f1_t[:, :, :], f1_bank[:, :].rearrange("p (k n) -> p k n", k=KD), ACT.Copy).then_inc(f1_t_ok, 1)

            def router_hidden(pe, m):
                pe.wait_ge(f1_t_ok, m + 1)
                for k in range(KD):
                    last = pe.matmul(router_bank[:, 0:2 * P], rw1[:, k, :], f1_t[:, k, :], start=k == 0, stop=k == KD - 1)
                last.then_inc(rh_ok, 1)

            def router_relu(act, m):
                act.wait_ge(rh_ok, m + 1)
                act.activation(rh_t[:, :], router_bank[:, 0:2 * P], ACT.Relu, bias=rb1[:, :]).then_inc(rh_t_ok, 1)

            def router_logits(pe, m):
                pe.wait_ge(rh_t_ok, m + 1)
                for h in range(2):
                    last = pe.matmul(router_bank[:, 256 + 8 * h:256 + 8 * h + EXPERTS], rh_t[:, h * P:(h + 1) * P], rw2[:, :],
                                     start=True, stop=True)
                last.then_inc(logit_ok, 1)

            ROUTE = 13

            def route_top(dve, m):
                at = ROUTE * m
                dve.wait_ge(logit_ok, m + 1)
                dve.tensor_tensor(logits[:, :, 0:EXPERTS], router_bank[:, 256:272].rearrange("p (h e) -> p h e", h=2)[:, :, 0:EXPERTS],
                                  rb2[:, :].unsqueeze(1).to_broadcast([P, 2, EXPERTS]), ALU.add).then_inc(route, 1)
                hold(dve, route, at + 1)
                for h in range(2):
                    dve.max(top[:, h, :], logits[:, h, :]).then_inc(route, 1)
                dve.wait_ge(route, at + 3)
                dve.tensor_tensor(less_top[:, :, :], logits[:, :, :], top[:, :, 0:1].to_broadcast([P, 2, 8]), ALU.subtract).then_inc(route, 1)

            def route_exp(act, m):
                act.wait_ge(route, ROUTE * m + 4)
                act.activation(exps[:, :, :], less_top[:, :, :], ACT.Exp).then_inc(route, 1)

            def route_probs(dve, m):
                at = ROUTE * m
                dve.wait_ge(route, at + 5)
                dve.tensor_reduce(norm[:, :, 0:1], exps[:, :, :], AX.X, ALU.add).then_inc(route, 1)
                dve.wait_ge(route, at + 6)
                dve.reciprocal(norm[:, :, 1:2], norm[:, :, 0:1]).then_inc(route, 1)
                dve.wait_ge(route, at + 7)
                dve.tensor_tensor(exps[:, :, :], exps[:, :, :], norm[:, :, 1:2].to_broadcast([P, 2, 8]), ALU.mult).then_inc(route, 1)
                hold(dve, route, at + 8)
                for h in range(2):
                    last = dve.max(top[:, h, :], exps[:, h, :])
                last.then_inc(route, 1)
                hold(dve, route, at + 9)
                for h in range(2):
                    last = dve.max_index(top_i[:, h, :], top[:, h, :], exps[:, h, :])
                last.then_inc(route, 1)
                dve.wait_ge(route, at + 10)
                dve.tensor_copy(top_f[:, :].rearrange("p (h t) -> p h t", h=2), top_i[:, :, 0:2])
                dve.tensor_tensor(norm[:, :, 0:1], top[:, :, 1:2], top[:, :, 0:1], ALU.subtract).then_inc(route, 1)

            def route_second(act, m):
                act.wait_ge(route, ROUTE * m + 11)
                act.activation(norm[:, :, 1:2], norm[:, :, 0:1], ACT.Exp).then_inc(route, 1)

            def route_shares(dve, m):
                at = ROUTE * m
                dve.wait_ge(route, at + 12)
                dve.tensor_scalar(norm[:, :, 0:1], norm[:, :, 1:2], 1.0, None, ALU.add).then_inc(route, 1)
                dve.wait_ge(route, at + 13)
                base = SHARE * m
                dve.reciprocal(norm[:, :, 0:1], norm[:, :, 0:1]).then_inc(share_ok, 1)
                dve.tensor_tensor(pick[:, :, :, :].rearrange("p h t e -> p (h t) e"),
                                  top_f[:, :].unsqueeze(2).to_broadcast([P, 4, 8]),
                                  iota[:, 0:8].unsqueeze(1).to_broadcast([P, 4, 8]), ALU.is_equal).then_inc(share_ok, 1)
                dve.wait_ge(share_ok, base + 2)
                dve.tensor_tensor(norm[:, :, 1:2], norm[:, :, 1:2], norm[:, :, 0:1], ALU.mult).then_inc(share_ok, 1)
                dve.wait_ge(share_ok, base + 3)
                for h in range(2):
                    last = dve.tensor_scalar(share[:, h, :], pick[:, h, 0, :], norm[:, h, 0:1], None, ALU.mult)
                last.then_inc(share_ok, 1)
                dve.wait_ge(share_ok, base + 4)
                for h in range(2):
                    last = dve.scalar_tensor_tensor(share[:, h, :], pick[:, h, 1, :], norm[:, h, 1:2], share[:, h, :], ALU.mult, ALU.add)
                last.then_inc(share_ok, 1)

            SHARE = 5

            def bias_turn(pe, m):
                pe.wait_ge(share_ok, SHARE * (m + 1))
                for h in range(2):
                    last = pe.transpose(router_bank[0:8, h * P:(h + 1) * P], share[:, h, :], ident[:, :])
                last.then_inc(share_turned, 1)

            def bias_turned(act, m):
                act.wait_ge(share_turned, m + 1)
                act.activation(share_t[:, :], router_bank[0:8, 0:2 * P], ACT.Copy).then_inc(share_t_ok, 1)

            def bias_product(pe, m):
                pe.wait_ge(share_t_ok, m + 1)
                for h in range(2):
                    last = pe.matmul(f1_bank[:, h * D:(h + 1) * D], share_t[0:EXPERTS, h * P:(h + 1) * P], eb3[:, :], start=True, stop=True)
                last.then_inc(bias_ok, 1)

            def bias_residual(dve, m):
                dve.wait_ge(bias_ok, m + 1)
                dve.wait_ge(mixed_free, m + 1)
                for h in range(2):
                    last = dve.tensor_tensor(mixed[:, h, :], f1_bank[:, h * D:(h + 1) * D], x1[h][:, :], ALU.add)
                last.then_inc(kept_ok[2], 1)

            def expert_up(pe, m, e):
                if e > 0:
                    pe.wait_ge(kept_ok[0], EXPERTS * m + e)
                for half in range(KD):
                    for k in range(KD):
                        last = pe.matmul(layer_bank[0][:, half * D:(half + 1) * D], ew1[:, e * KD + k, half * P:(half + 1) * P],
                                         f1_t[:, k, :], start=k == 0, stop=k == KD - 1)
                last.then_inc(made_ok[0], 1)

            def expert_relu(act, m, e, layer):
                act.wait_ge(made_ok[layer], EXPERTS * m + e + 1)
                to, bias = ((h1_t[e % 2], eb1), (h2_t[e % 2], eb2))[layer]
                for half in range(KD):
                    last = act.activation(to[:, half, :], layer_bank[layer][:, half * D:(half + 1) * D], ACT.Relu,
                                          bias=bias[:, e * KD + half:e * KD + half + 1])
                last.then_inc(kept_ok[layer], 1)

            def expert_mid(pe, m, e):
                pe.wait_ge(kept_ok[0], EXPERTS * m + e + 1)
                if e > 0:
                    pe.wait_ge(kept_ok[1], EXPERTS * m + e)
                for half in range(KD):
                    for k in range(KD):
                        last = pe.matmul(layer_bank[1][:, half * D:(half + 1) * D], ew2[:, e * KD + k, half * P:(half + 1) * P],
                                         h1_t[e % 2][:, k, :], start=k == 0, stop=k == KD - 1)
                last.then_inc(made_ok[1], 1)

            def down_bank(e):
                return f1_bank if e % 2 else layer_bank[2]

            def expert_down(pe, m, e):
                pe.wait_ge(kept_ok[1], EXPERTS * m + e + 1)
                if e > 0:
                    pe.wait_ge(kept_ok[2], (EXPERTS + 1) * m + e)
                for h in range(2):
                    for k in range(KD):
                        last = pe.matmul(down_bank(e)[:, h * D:(h + 1) * D], h2_t[e % 2][:, k, h * P:(h + 1) * P], ew3[:, e * KD + k, :],
                                         start=k == 0, stop=k == KD - 1)
                last.then_inc(made_ok[2], 1)

            def expert_add(dve, m, e):
                dve.wait_ge(made_ok[2], EXPERTS * m + e + 1)
                dve.wait_ge(kept_ok[2], (EXPERTS + 1) * m + e + 1)
                for h in range(2):
                    last = dve.scalar_tensor_tensor(mixed[:, h, :], down_bank(e)[:, h * D:(h + 1) * D], share[:, h, e:e + 1],
                                                    mixed[:, h, :], ALU.mult, ALU.add)
                last.then_inc(kept_ok[2], 1)

            def moe_store(sp, m, g, credit=0):
                sp.wait_ge(kept_ok[2], (EXPERTS + 1) * (m + 1))
                sp.dma_start(x_rows(out_g, g), mixed[:, :, :]).then_inc(out_stored, 16)
                sp.wait_ge(out_stored, 16 * (m + 1 - credit))
                sp.sem_inc(mixed_free, 1)

            def x_load(sp, n, g, first):
                if not first:
                    sp.wait_ge(x1_ok[1], n)
                sp.dma_start(x_in[:, :, :], x_rows(x_g, g)).then_inc(x_loaded, 16)

            with nc.Block() as block:
                @block.sync
                def _(sp):
                    def by_windows():
                        def windows_of(g, first):
                            for h in range(2):
                                start = sp.value_load(starts[0:1, bass.ds(2 * g + h, 1)], min_val=0, max_val=n_edges)
                                window_load(sp, start, h, g, first)

                        sp.sem_inc(mixed_free, 1)
                        windows_of(0, True)
                        x_load(sp, 0, 0, True)
                        windows_of(1, False)
                        x_load(sp, 1, 1, False)
                        with sp.Fori(1, groups - 1) as g:
                            windows_of(g + 1, False)
                            moe_store(sp, g - 1, g - 1)
                            x_load(sp, g + 1, g + 1, False)
                        moe_store(sp, groups - 2, groups - 2)
                        moe_store(sp, groups - 1, groups - 1)

                    def any_edges():
                        sp.sem_inc(mixed_free, 2)
                        with sp.Fori(0, groups) as g:
                            x_load(sp, g + 1, g, False)
                            for h in range(2):
                                with sp.Fori(0, all_windows) as w:
                                    window_load(sp, w * WIN, h, g * all_windows + w + 1, False)
                            moe_store(sp, g + 1, g, 1)

                    fit = sp.value_load(fits[0:1, 0:1], min_val=0, max_val=1)
                    with sp.If(fit == 1):
                        by_windows()
                    with sp.Else():
                        any_edges()

                @block.gpsimd
                def _(gp):
                    def by_windows():
                        for h in range(2):
                            window_gather(gp, h, 0, True)
                        with gp.Fori(1, groups) as g:
                            for h in range(2):
                                window_gather(gp, h, g, False)

                    def any_edges():
                        with gp.Fori(0, groups) as g:
                            for h in range(2):
                                with gp.Fori(0, all_windows) as w:
                                    window_gather(gp, h, g * all_windows + w + 1, False, 1)

                    fit = gp.value_load(fits[0:1, 0:1], min_val=0, max_val=1)
                    with gp.If(fit == 1):
                        by_windows()
                    with gp.Else():
                        any_edges()

                @block.tensor
                def _(pe):
                    def experts(m):
                        moe_turn(pe, m)
                        router_hidden(pe, m)
                        router_logits(pe, m)
                        expert_up(pe, m, 0)
                        expert_up(pe, m, 1)
                        expert_mid(pe, m, 0)
                        bias_turn(pe, m)
                        expert_up(pe, m, 2)
                        bias_product(pe, m)
                        expert_mid(pe, m, 1)
                        expert_down(pe, m, 0)
                        for e in range(3, EXPERTS):
                            expert_up(pe, m, e)
                            expert_mid(pe, m, e - 1)
                            expert_down(pe, m, e - 2)
                        expert_mid(pe, m, EXPERTS - 1)
                        expert_down(pe, m, EXPERTS - 2)
                        expert_down(pe, m, EXPERTS - 1)

                    def by_windows():
                        def window(g, h):
                            for sub in range(SUBS):
                                for half in range(2):
                                    window_add(pe, h, g, sub, half)

                        for h in range(2):
                            window(0, h)
                        with pe.Fori(1, groups) as g:
                            m = g - 1
                            pe.wait_ge(x1_ok[0], g)
                            window_add(pe, 0, g, 0, 0)
                            window_add(pe, 0, g, 0, 1)
                            window_add(pe, 0, g, 1, 0)
                            moe_turn(pe, m)
                            window_add(pe, 0, g, 1, 1)
                            router_hidden(pe, m)
                            window_add(pe, 0, g, 2, 0)
                            router_logits(pe, m)
                            expert_up(pe, m, 0)
                            window_add(pe, 0, g, 2, 1)
                            expert_up(pe, m, 1)
                            expert_mid(pe, m, 0)
                            expert_up(pe, m, 2)
                            bias_turn(pe, m)
                            expert_mid(pe, m, 1)
                            bias_product(pe, m)
                            expert_up(pe, m, 3)
                            expert_down(pe, m, 0)
                            pe.wait_ge(x1_ok[1], g)
                            window_add(pe, 1, g, 0, 0)
                            expert_mid(pe, m, 2)
                            window_add(pe, 1, g, 0, 1)
                            expert_down(pe, m, 1)
                            window_add(pe, 1, g, 1, 0)
                            expert_up(pe, m, 4)
                            expert_mid(pe, m, 3)
                            window_add(pe, 1, g, 1, 1)
                            expert_down(pe, m, 2)
                            expert_up(pe, m, 5)
                            window_add(pe, 1, g, 2, 0)
                            expert_mid(pe, m, 4)
                            expert_down(pe, m, 3)
                            window_add(pe, 1, g, 2, 1)
                            expert_mid(pe, m, 5)
                            expert_down(pe, m, 4)
                            expert_down(pe, m, 5)
                        experts(groups - 1)

                    def any_edges():
                        for h in range(2):
                            pe.sem_inc(used[h], SUBS)
                        for semaphore, worth in ((f1_turned, 1), (rh_ok, 1), (logit_ok, 1), (share_turned, 1), (bias_ok, 1),
                                                 (made_ok[0], EXPERTS), (made_ok[1], EXPERTS), (made_ok[2], EXPERTS)):
                            pe.sem_inc(semaphore, worth)
                        with pe.Fori(0, groups) as g:
                            for h in range(2):
                                with pe.Fori(0, all_windows) as w:
                                    n = g * all_windows + w + 1
                                    pe.wait_ge(added[h], n)
                                    for sub in range(SUBS):
                                        for half in range(2):
                                            window_add(pe, h, n, sub, half)
                            experts(g + 1)

                    fit = pe.value_load(fits[0:1, 0:1], min_val=0, max_val=1)
                    with pe.If(fit == 1):
                        by_windows()
                    with pe.Else():
                        any_edges()

                @block.scalar
                def _(act):
                    def experts(m):
                        moe_turned(act, m)
                        router_relu(act, m)
                        route_exp(act, m)
                        expert_relu(act, m, 0, 0)
                        expert_relu(act, m, 1, 0)
                        route_second(act, m)
                        expert_relu(act, m, 0, 1)
                        bias_turned(act, m)
                        for e in range(2, EXPERTS):
                            expert_relu(act, m, e, 0)
                            expert_relu(act, m, e - 1, 1)
                        expert_relu(act, m, EXPERTS - 1, 1)

                    def by_windows():
                        for h in range(2):
                            window_exp(act, h, 0)
                            graph_root(act, h, 0)
                        def step(g, more):
                            m = g - 1
                            moe_turned(act, m)
                            router_relu(act, m)
                            route_exp(act, m)
                            expert_relu(act, m, 0, 0)
                            expert_relu(act, m, 1, 0)
                            route_second(act, m)
                            expert_relu(act, m, 0, 1)
                            bias_turned(act, m)
                            expert_relu(act, m, 2, 0)
                            window_exp(act, 1, g)
                            expert_relu(act, m, 1, 1)
                            expert_relu(act, m, 3, 0)
                            graph_root(act, 0, g)
                            expert_relu(act, m, 2, 1)
                            expert_relu(act, m, 4, 0)
                            expert_relu(act, m, 3, 1)
                            expert_relu(act, m, 5, 0)
                            expert_relu(act, m, 4, 1)
                            if more:
                                window_exp(act, 0, g + 1)
                            expert_relu(act, m, 5, 1)
                            graph_root(act, 1, g)

                        window_exp(act, 0, 1)
                        with act.Fori(1, groups - 1) as g:
                            step(g, True)
                        step(groups - 1, False)
                        experts(groups - 1)

                    def any_edges():
                        for h in range(2):
                            for semaphore in (exp_ok[h], std_ok[h]):
                                act.sem_inc(semaphore, 1)
                        for semaphore, worth in ((f1_t_ok, 1), (rh_t_ok, 1), (share_t_ok, 1), (kept_ok[0], EXPERTS), (kept_ok[1], EXPERTS)):
                            act.sem_inc(semaphore, worth)
                        with act.Fori(0, groups) as g:
                            for h in range(2):
                                with act.Fori(0, all_windows) as w:
                                    window_exp(act, h, g * all_windows + w + 1)
                                graph_root(act, h, g + 1)
                            experts(g + 1)

                    fit = act.value_load(fits[0:1, 0:1], min_val=0, max_val=1)
                    with act.If(fit == 1):
                        by_windows()
                    with act.Else():
                        any_edges()

                @block.vector
                def _(dve):
                    def experts(m):
                        route_top(dve, m)
                        route_probs(dve, m)
                        route_shares(dve, m)
                        bias_residual(dve, m)
                        for e in range(EXPERTS):
                            expert_add(dve, m, e)

                    def by_windows():
                        def weights(g, h, first):
                            b = 2 * g + h
                            window_weights(dve, h, g, first, b, b * SLOTS)
                            window_alpha(dve, h, g)

                        def block_norm(h, g):
                            graph_norm(dve, h, g, agg_bank[h][:, 0:D], used[h], SUBS * (g + 1))

                        for h in range(2):
                            weights(0, h, True)
                            for sub in range(SUBS):
                                window_hot(dve, h, sub)
                            block_norm(h, 0)
                            graph_features(dve, h, 0)
                        def step(g, more):
                            m = g - 1
                            route_top(dve, m)
                            route_probs(dve, m)
                            route_shares(dve, m)
                            bias_residual(dve, m)
                            weights(g, 1, False)
                            window_hot(dve, 1, 0)
                            expert_add(dve, m, 0)
                            block_norm(0, g)
                            window_hot(dve, 1, 1)
                            expert_add(dve, m, 1)
                            window_hot(dve, 1, 2)
                            graph_features(dve, 0, g)
                            expert_add(dve, m, 2)
                            expert_add(dve, m, 3)
                            if more:
                                weights(g + 1, 0, False)
                                window_hot(dve, 0, 0)
                            expert_add(dve, m, 4)
                            block_norm(1, g)
                            if more:
                                window_hot(dve, 0, 1)
                            expert_add(dve, m, 5)
                            graph_features(dve, 1, g)
                            if more:
                                window_hot(dve, 0, 2)

                        weights(1, 0, False)
                        for sub in range(SUBS):
                            window_hot(dve, 0, sub)
                        with dve.Fori(1, groups - 1) as g:
                            step(g, True)
                        step(groups - 1, False)
                        experts(groups - 1)

                    def any_edges():
                        for h in range(2):
                            for semaphore in (local_ok[h], diff_ok[h], min_ok[h], alpha_ok[h], res_ok[h], x1_ok[h],
                                              stats_ok[h], moments_ok[h], var_ok[h], rstd_ok[h], f1_ok[h], added[h]):
                                dve.sem_inc(semaphore, 1)
                            dve.sem_inc(hot_ok[h], SUBS)
                        for semaphore, worth in ((route, ROUTE), (share_ok, SHARE), (kept_ok[2], EXPERTS + 1)):
                            dve.sem_inc(semaphore, worth)
                        with dve.Fori(0, groups) as g:
                            for h in range(2):
                                dve.memset(agg[h][:, :], 0.0).then_inc(cleared, 1)
                                hold(dve, cleared, 2 * g + h + 1)
                                with dve.Fori(0, all_windows) as w:
                                    n = g * all_windows + w + 1
                                    window_weights(dve, h, n, False, 2 * g + h, w * SLOTS, 1)
                                    window_alpha(dve, h, n)
                                    for sub in range(SUBS):
                                        window_hot(dve, h, sub)
                                    dve.wait_ge(used[h], SUBS * (n + 1))
                                    dve.wait_ge(added[h], n)
                                    dve.tensor_tensor(agg[h][:, :], agg[h][:, :], agg_bank[h][:, 0:D], ALU.add).then_inc(added[h], 1)
                                graph_norm(dve, h, g + 1, agg[h][:, :], added[h], (g + 1) * all_windows + 1, 1)
                                graph_features(dve, h, g + 1)
                            experts(g + 1)

                    dve.memset(logits[:, :, :], -BIG)
                    fit = dve.value_load(fits[0:1, 0:1], min_val=0, max_val=1)
                    with dve.If(fit == 1):
                        by_windows()
                    with dve.Else():
                        any_edges()


def layout(inputs):
    import numpy as np

    def c(v):
        return np.ascontiguousarray(v)

    x, src, dst = inputs["x"], inputs["src"], inputs["dst"]
    padded = -(-x.shape[0] // (2 * P)) * 2 * P
    no_node = np.full(WIN, 1 << 20, dst.dtype)
    arrays = {
        "x": c(np.concatenate([x, np.zeros((padded - x.shape[0], D), x.dtype)])),
        "src": c(np.concatenate([src, np.zeros(WIN, src.dtype)])),
        "dst": c(np.concatenate([dst, no_node])),
        "w_st": c(np.concatenate([inputs["L0_gnn_W_s"].T, inputs["L0_gnn_W_t"].T], axis=1)),
        "w_attn": c(inputs["L0_gnn_W_attn"].reshape(-1)),
        "w_fc": c(inputs["L0_gnn_W_fc"].T),
        "b_fc": c(inputs["L0_gnn_b_fc"]),
        "rw1": c(inputs["L0_ffn_router_w1"]),
        "rb1": c(inputs["L0_ffn_router_b1"].reshape(-1, 1)),
        "rw2": c(inputs["L0_ffn_router_w2"]),
        "rb2": c(inputs["L0_ffn_router_b2"]),
        "ew1": c(inputs["L0_ffn_expert_w1"]),
        "ew2": c(inputs["L0_ffn_expert_w2"]),
        "ew3": c(inputs["L0_ffn_expert_w3"]),
        "eb1": c(inputs["L0_ffn_expert_b1"].reshape(EXPERTS * KD, P).T),
        "eb2": c(inputs["L0_ffn_expert_b2"].reshape(EXPERTS * KD, P).T),
        "eb3": c(inputs["L0_ffn_expert_b3"]),
    }
    return arrays, src.shape[0], padded


def kernel(**inputs):
    import numpy as np
    import concourse.bacc as bacc
    from concourse import mybir as mb
    from concourse.bass_utils import run_bass_kernel_spmd

    arrays, n_edges, padded = layout({k: np.asarray(v) for k, v in inputs.items()})
    nc = bacc.Bacc("TRN2", target_bir_lowering=False, num_devices=1)
    a = {k: nc.dram_tensor("in_" + k, v.shape, mb.dt.from_np(v.dtype), kind="ExternalInput").ap() for k, v in arrays.items()}
    out = nc.dram_tensor("out_x", [padded, D], F32, kind="ExternalOutput").ap()
    a["n_edges"] = n_edges
    gat_moe(nc, a, out)
    r = run_bass_kernel_spmd(nc, [{"in_" + k: v for k, v in arrays.items()}], core_ids=[0])
    return r.results[0]["out_x"][:inputs["x"].shape[0]]
```
